# Optimizing a Trainium2 kernel written in Bass

```python
import numpy as np
import jax
import jax.numpy as jnp

def _softmax(x, axis=-1):
    return jax.nn.softmax(x, axis=axis)

def _gelu(x):
    return jax.nn.gelu(x, approximate=True)

def _silu(x):
    return jax.nn.silu(x)

def _sigmoid(x):
    return jax.nn.sigmoid(x)

def _layernorm(x, axis=-1, eps=1e-05):
    m = jnp.mean(x, axis=axis, keepdims=True)
    v = jnp.var(x, axis=axis, keepdims=True)
    return (x - m) / jnp.sqrt(v + eps)

def _scatter_add(tgt, idx, src, axis=0):
    return tgt.at[idx].add(src)

def _segment_sum(src, seg, n):
    return jax.ops.segment_sum(src, seg, n)
kernel_name = 'mk_xattn_seq_d2_seqx_r4_9bab84'

def setup_inputs(seed: int=0):
    np.random.seed(seed)
    _w = jnp.asarray

    def _rec_inputs():
        import jax
        import jax.numpy as jnp
        _rk = jax.random.key(seed)
        x = -0.0002928 + 1 * jax.random.normal(jax.random.fold_in(_rk, 1), (8, 256, 256), jnp.float32)
        _lenS = 256 - jax.random.randint(jax.random.fold_in(_rk, 7), (8,), 0, max(1, 256 // 4) + 1, jnp.int32)
        _lenS2 = 77 - jax.random.randint(jax.random.fold_in(_rk, 8), (8,), 0, max(1, 77 // 4) + 1, jnp.int32)
        _ctx_768P = jax.random.normal(jax.random.fold_in(_rk, 11), (8, 16, 192), jnp.float32)
        _ctx_768c = jax.random.dirichlet(jax.random.fold_in(_rk, 511), 0.3 * jnp.ones((16,), jnp.float32), (8, 77))
        _ctx_768t = jnp.einsum('bsk,bkd->bsd', _ctx_768c, _ctx_768P)
        _ctx_768t = _ctx_768t * jax.lax.rsqrt(jnp.mean(jnp.square(_ctx_768t)) + 1e-12) * 0.953939
        ctx_768 = -0.00055796 + 0.999787 * (_ctx_768t + 0.3 * jax.random.normal(jax.random.fold_in(_rk, 611), (8, 77, 192), jnp.float32))
        _validS = jnp.arange(256)[None, :] < _lenS[:, None]
        _validS2 = jnp.arange(77)[None, :] < _lenS2[:, None]
        _causal = jnp.tril(jnp.ones((256, 256), dtype=bool))
        mask_BxS2_if1 = jnp.where(jnp.ones((8, 77), dtype=bool), 1, 0).astype(jnp.int32)
        return (x, ctx_768, mask_BxS2_if1)
    x, ctx_768, mask_BxS2_if1 = _rec_inputs()

    def _L0_xattn_setup():
        import jax, jax.numpy as jnp
        import numpy as np
        DEPTH = 4
        DIM = 256
        HEADS = 16
        DIM_HEAD = 64
        INNER = HEADS * DIM_HEAD
        MLP = 1024
        CTX = 192
        SCALE = DIM_HEAD ** (-0.5)
        EPS = 1e-05

        def _ln(x, g, b):
            mu = jnp.mean(x, axis=-1, keepdims=True)
            var = jnp.mean(jnp.square(x - mu), axis=-1, keepdims=True)
            return (x - mu) * jax.lax.rsqrt(var + EPS) * g + b

        def _heads(t):
            b, n, _ = t.shape
            return t.reshape(b, n, HEADS, DIM_HEAD).transpose(0, 2, 1, 3)

        def _mha(q, k, v):
            attn = jax.nn.softmax(jnp.einsum('bhqd,bhkd->bhqk', q, k) * SCALE, axis=-1)
            out = jnp.einsum('bhqk,bhkd->bhqd', attn, v)
            b, h, n, d = out.shape
            return out.transpose(0, 2, 1, 3).reshape(b, n, h * d)
        key = jax.random.key(seed)
        ks = jax.random.split(key, 12)

        def rn(k, shape, s=0.02):
            return jax.random.normal(k, shape, jnp.float32) * s
        return {'x': jax.random.normal(ks[0], (2, 512, DIM), jnp.float32), 'context': jax.random.normal(ks[1], (2, 256, CTX), jnp.float32), 'ln1_g': jnp.ones((DEPTH, DIM), jnp.float32), 'ln1_b': jnp.zeros((DEPTH, DIM), jnp.float32), 'w_qkv': rn(ks[2], (DEPTH, DIM, 3 * INNER)), 'w_sa_o': rn(ks[3], (DEPTH, INNER, DIM)), 'b_sa_o': jnp.zeros((DEPTH, DIM), jnp.float32), 'ln2_g': jnp.ones((DEPTH, DIM), jnp.float32), 'ln2_b': jnp.zeros((DEPTH, DIM), jnp.float32), 'w_q': rn(ks[4], (DEPTH, DIM, INNER)), 'w_kv': rn(ks[5], (DEPTH, CTX, 2 * INNER)), 'w_ca_o': rn(ks[6], (DEPTH, INNER, DIM)), 'b_ca_o': jnp.zeros((DEPTH, DIM), jnp.float32), 'ln3_g': jnp.ones((DEPTH, DIM), jnp.float32), 'ln3_b': jnp.zeros((DEPTH, DIM), jnp.float32), 'w_ff1': rn(ks[7], (DEPTH, DIM, MLP)), 'b_ff1': jnp.zeros((DEPTH, MLP), jnp.float32), 'w_ff2': rn(ks[8], (DEPTH, MLP, DIM)), 'b_ff2': jnp.zeros((DEPTH, DIM), jnp.float32)}
    _L0_xattn_all = _L0_xattn_setup()
    _L0_xattn_in = {k: v for k, v in _L0_xattn_all.items() if k in ('ln1_g', 'ln1_b', 'w_qkv', 'w_sa_o', 'b_sa_o', 'ln2_g', 'ln2_b', 'w_q', 'w_kv', 'w_ca_o', 'b_ca_o', 'ln3_g', 'ln3_b', 'w_ff1', 'b_ff1', 'w_ff2', 'b_ff2')}
    del _L0_xattn_all

    def _L1_xattn_setup():
        import jax, jax.numpy as jnp
        import numpy as np
        import math
        H = 8
        D = 256
        D_I = 256
        D_L = 192
        EPS = 1e-05
        key = jax.random.key(seed)
        ks = jax.random.split(key, 8)
        B, NQ, NK = (8, 196, 128)
        img_embed = jax.random.normal(ks[0], (B, NQ, D_I), dtype=jnp.float32)
        sent_embed = jax.random.normal(ks[1], (B, NK, D_L), dtype=jnp.float32)
        atten_mask = jnp.ones((B, NK), dtype=jnp.int32)
        Wq = jax.random.normal(ks[2], (D_I, H * D), dtype=jnp.float32) * (1.0 / math.sqrt(D_I))
        Wk = jax.random.normal(ks[3], (D_L, H * D), dtype=jnp.float32) * (1.0 / math.sqrt(D_L))
        Wv = jax.random.normal(ks[4], (D_L, H * D), dtype=jnp.float32) * (1.0 / math.sqrt(D_L))
        Wo = jax.random.normal(ks[5], (H * D, D_I), dtype=jnp.float32) * (1.0 / math.sqrt(H * D))
        gamma = jnp.ones((D_I,), dtype=jnp.float32)
        beta = jnp.zeros((D_I,), dtype=jnp.float32)
        return {'img_embed': img_embed, 'sent_embed': sent_embed, 'atten_mask': atten_mask, 'Wq': Wq, 'Wk': Wk, 'Wv': Wv, 'Wo': Wo, 'gamma': gamma, 'beta': beta}
    _L1_xattn_all = _L1_xattn_setup()
    _L1_xattn_in = {k: v for k, v in _L1_xattn_all.items() if k in ('Wq', 'Wk', 'Wv', 'Wo', 'gamma', 'beta')}
    del _L1_xattn_all
    return {'x': x, 'ctx_768': ctx_768, 'mask_BxS2_if1': mask_BxS2_if1, 'L0_xattn_ln1_g': _L0_xattn_in['ln1_g'], 'L0_xattn_ln1_b': _L0_xattn_in['ln1_b'], 'L0_xattn_w_qkv': _L0_xattn_in['w_qkv'], 'L0_xattn_w_sa_o': _L0_xattn_in['w_sa_o'], 'L0_xattn_b_sa_o': _L0_xattn_in['b_sa_o'], 'L0_xattn_ln2_g': _L0_xattn_in['ln2_g'], 'L0_xattn_ln2_b': _L0_xattn_in['ln2_b'], 'L0_xattn_w_q': _L0_xattn_in['w_q'], 'L0_xattn_w_kv': _L0_xattn_in['w_kv'], 'L0_xattn_w_ca_o': _L0_xattn_in['w_ca_o'], 'L0_xattn_b_ca_o': _L0_xattn_in['b_ca_o'], 'L0_xattn_ln3_g': _L0_xattn_in['ln3_g'], 'L0_xattn_ln3_b': _L0_xattn_in['ln3_b'], 'L0_xattn_w_ff1': _L0_xattn_in['w_ff1'], 'L0_xattn_b_ff1': _L0_xattn_in['b_ff1'], 'L0_xattn_w_ff2': _L0_xattn_in['w_ff2'], 'L0_xattn_b_ff2': _L0_xattn_in['b_ff2'], 'L1_xattn_Wq': _L1_xattn_in['Wq'], 'L1_xattn_Wk': _L1_xattn_in['Wk'], 'L1_xattn_Wv': _L1_xattn_in['Wv'], 'L1_xattn_Wo': _L1_xattn_in['Wo'], 'L1_xattn_gamma': _L1_xattn_in['gamma'], 'L1_xattn_beta': _L1_xattn_in['beta']}

def reference(x, ctx_768, mask_BxS2_if1, L0_xattn_ln1_g, L0_xattn_ln1_b, L0_xattn_w_qkv, L0_xattn_w_sa_o, L0_xattn_b_sa_o, L0_xattn_ln2_g, L0_xattn_ln2_b, L0_xattn_w_q, L0_xattn_w_kv, L0_xattn_w_ca_o, L0_xattn_b_ca_o, L0_xattn_ln3_g, L0_xattn_ln3_b, L0_xattn_w_ff1, L0_xattn_b_ff1, L0_xattn_w_ff2, L0_xattn_b_ff2, L1_xattn_Wq, L1_xattn_Wk, L1_xattn_Wv, L1_xattn_Wo, L1_xattn_gamma, L1_xattn_beta):
    import jax
    import jax.numpy as jnp

    def _L0_xattn_ref(x, context, ln1_g, ln1_b, w_qkv, w_sa_o, b_sa_o, ln2_g, ln2_b, w_q, w_kv, w_ca_o, b_ca_o, ln3_g, ln3_b, w_ff1, b_ff1, w_ff2, b_ff2):
        import jax, jax.numpy as jnp
        import numpy as np
        DEPTH = 4
        DIM = 256
        HEADS = 16
        DIM_HEAD = 64
        INNER = HEADS * DIM_HEAD
        MLP = 1024
        CTX = 192
        SCALE = DIM_HEAD ** (-0.5)
        EPS = 1e-05

        def _ln(x, g, b):
            mu = jnp.mean(x, axis=-1, keepdims=True)
            var = jnp.mean(jnp.square(x - mu), axis=-1, keepdims=True)
            return (x - mu) * jax.lax.rsqrt(var + EPS) * g + b

        def _heads(t):
            b, n, _ = t.shape
            return t.reshape(b, n, HEADS, DIM_HEAD).transpose(0, 2, 1, 3)

        def _mha(q, k, v):
            attn = jax.nn.softmax(jnp.einsum('bhqd,bhkd->bhqk', q, k) * SCALE, axis=-1)
            out = jnp.einsum('bhqk,bhkd->bhqd', attn, v)
            b, h, n, d = out.shape
            return out.transpose(0, 2, 1, 3).reshape(b, n, h * d)
        for i in range(DEPTH):
            h = _ln(x, ln1_g[i], ln1_b[i])
            qkv = h @ w_qkv[i]
            q, k, v = jnp.split(qkv, 3, axis=-1)
            sa = _mha(_heads(q), _heads(k), _heads(v)) @ w_sa_o[i] + b_sa_o[i]
            x = sa + x
            h = _ln(x, ln2_g[i], ln2_b[i])
            q = h @ w_q[i]
            kv = context @ w_kv[i]
            k, v = jnp.split(kv, 2, axis=-1)
            ca = _mha(_heads(q), _heads(k), _heads(v)) @ w_ca_o[i] + b_ca_o[i]
            x = ca + x
            h = _ln(x, ln3_g[i], ln3_b[i])
            ff = jax.nn.gelu(h @ w_ff1[i] + b_ff1[i], approximate=False) @ w_ff2[i] + b_ff2[i]
            x = ff + x
        return x

    def _L1_xattn_ref(img_embed, sent_embed, atten_mask, Wq, Wk, Wv, Wo, gamma, beta):
        import jax, jax.numpy as jnp
        import numpy as np
        import math
        H = 8
        D = 256
        D_I = 256
        D_L = 192
        EPS = 1e-05
        B = img_embed.shape[0]
        Q = (img_embed @ Wq).reshape(B, -1, H, D).transpose(0, 2, 1, 3)
        K = (sent_embed @ Wk).reshape(B, -1, H, D).transpose(0, 2, 1, 3)
        V = (sent_embed @ Wv).reshape(B, -1, H, D).transpose(0, 2, 1, 3)
        score = jnp.einsum('bhqd,bhkd->bhqk', Q, K) / math.sqrt(D)
        mask = (atten_mask != 0)[:, None, None, :]
        score = jnp.where(mask, score, -jnp.inf)
        attn = jax.nn.softmax(score, axis=-1)
        ctx = jnp.einsum('bhqk,bhkd->bqhd', attn, V).reshape(B, -1, H * D)
        out = ctx @ Wo + img_embed
        mu = jnp.mean(out, axis=-1, keepdims=True)
        var = jnp.var(out, axis=-1, keepdims=True)
        return (out - mu) * jax.lax.rsqrt(var + EPS) * gamma + beta
    x = _L0_xattn_ref(x, ctx_768, L0_xattn_ln1_g, L0_xattn_ln1_b, L0_xattn_w_qkv, L0_xattn_w_sa_o, L0_xattn_b_sa_o, L0_xattn_ln2_g, L0_xattn_ln2_b, L0_xattn_w_q, L0_xattn_w_kv, L0_xattn_w_ca_o, L0_xattn_b_ca_o, L0_xattn_ln3_g, L0_xattn_ln3_b, L0_xattn_w_ff1, L0_xattn_b_ff1, L0_xattn_w_ff2, L0_xattn_b_ff2)
    x = _L1_xattn_ref(x, ctx_768, mask_BxS2_if1, L1_xattn_Wq, L1_xattn_Wk, L1_xattn_Wv, L1_xattn_Wo, L1_xattn_gamma, L1_xattn_beta)
    return x

_drawn_inputs = setup_inputs


def setup_inputs(seed=0):
    import zlib

    import numpy as np

    out = dict(_drawn_inputs(seed))
    spreads = {'L0_xattn_ln1_g': (1.0, 0.6),
     'L0_xattn_ln1_b': (0.0, 0.1),
     'L0_xattn_b_sa_o': (0.0, 0.1),
     'L0_xattn_ln2_g': (1.0, 0.6),
     'L0_xattn_ln2_b': (0.0, 0.8),
     'L0_xattn_b_ca_o': (0.0, 0.1),
     'L0_xattn_ln3_g': (1.0, 0.2),
     'L0_xattn_ln3_b': (0.0, 0.414),
     'L0_xattn_b_ff1': (0.0, 0.1),
     'L0_xattn_b_ff2': (0.0, 0.1),
     'L1_xattn_gamma': (1.0, 0.2),
     'L1_xattn_beta': (0.0, 0.1)}
    factors = {'L0_xattn_w_q': 8.0}
    for name, (base, spread) in spreads.items():
        noise = np.random.default_rng([zlib.crc32(name.encode()), seed]).standard_normal(out[name].shape)
        drawn = base * np.exp(spread * noise) if base else spread * noise
        out[name] = jnp.asarray(drawn.astype(out[name].dtype))
    for name, factor in factors.items():
        out[name] = (out[name] * factor).astype(out[name].dtype)
    return out
```

```python
from contextlib import ExitStack

import concourse.bass as bass
from concourse import mybir

F32 = mybir.dt.float32
F32R = mybir.dt.float32r
I32 = mybir.dt.int32
ALU = mybir.AluOpType
ACT = mybir.ActivationFunctionType
AX = mybir.AxisListType

P = 128
L = 4
B = 8
S = 256
C = 256
H = 16
D = 64
KC = 77
KP = 78
HF = 8
EPS = 1e-5
SCALE = D ** -0.5
SCALE_F = 256 ** -0.5
NPAIR = H // 2
CH = 1024
NA_LOW, NB, NC, NA_HIGH = 4, 8, 4, 4
PER_LAYER = NA_LOW + NB + NC + NA_HIGH
NSTREAM = NA_HIGH + L * PER_LAYER
NCHUNK = NSTREAM + 12
CW = (B + 1) * KP
USES = 13
PRE = 3
A_USES = PRE + USES * B
B_USES = 1 + NPAIR * B
LAYER_USES = A_USES + B_USES + B + 1
V_USES = 5
V_OF = [1, 2, 3, 5]
O_AT = 0
QK_AT = [4 * CH, 5 * CH, 6 * CH, 2 * CH]
V_AT = [7 * CH, 7 * CH + 512, 3 * CH, 3 * CH + 512]
LOW_ORDER = [0, 3, 2, 1]
A_USE = {0: ("qk", 1), 2: ("qk", 2), 3: ("v", 1), 4: ("qk", 3), 6: ("qk", 4), 7: ("v", 2), 8: ("qk", 5),
         10: ("qk", 6), 11: ("v", 3), 12: ("qk", 7), 13: ("ln", 0), 14: ("qk", 0), 15: ("v", 0)}
A_NTH = {h: i for i, h in enumerate(sorted(A_USE))}
A_OF = {u: A_NTH[h] for h, u in A_USE.items()}


def build(nc, x, ctx_t, mask, wts, par, rows, rows_f, out):
    with ExitStack() as ctx:
        def sb(name, shape, dt=F32):
            return ctx.enter_context(nc.sbuf_tensor(name, shape, dt))

        def sem(name):
            return ctx.enter_context(nc.semaphore(name))

        w0h, w0l = sb("w0h", [P, 8 * CH], F32R), sb("w0l", [P, 8 * CH], F32R)
        w1h, w1l = sb("w1h", [P, 8 * CH], F32R), sb("w1l", [P, 8 * CH], F32R)
        staged = sb("staged", [P, CH])
        xres = sb("xres", [P, B + 1, 2, C])
        norm = sb("norm", [P, 2, C])
        htr = norm
        hTh, hTl = sb("hTh", [P, 2, S], F32R), sb("hTl", [P, 2, S], F32R)
        qkh, qkl = sb("qkh", [P, 2, 512], F32R), sb("qkl", [P, 2, 512], F32R)
        vhl = sb("vhl", [P, 2, 2, 4, 128], F32R)
        prob = sb("prob", [P, 2, 512])
        pth, ptl = sb("pth", [P, 2, 512], F32R), sb("ptl", [P, 2, 512], F32R)
        part = sb("part", [P, S])
        otr = sb("otr", [P, 2, S])
        oth, otl = sb("oth", [P, 2, S], F32R), sb("otl", [P, 2, S], F32R)
        cTh, cTl = sb("cTh", [P, 2, CW], F32R), sb("cTl", [P, 2, CW], F32R)
        brow = sb("brow", [P, 3, C])
        pk = sb("pk", [P, 20])
        ident = sb("ident", [P, P])
        stats = sb("stats", [P, 2, 6])
        mv = sb("mv", [P, 2, 2])
        vare = sb("vare", [P, 2])
        rstd = sb("rstd", [P, 2])
        half = sb("half", [P, 2])
        ones = sb("ones", [P, 1])
        eps = sb("eps", [P, 1])
        pace = sb("pace", [P, 1])
        nmax = sb("nmax", [P, 2, 4])
        nbias = sb("nbias", [P, 2, 4])
        psums = sb("psums", [P, 2, 4])
        rsum = sb("rsum", [P, 2, 4])

        sc = [ctx.enter_context(nc.psum_tensor(f"sc{i}", [P, 512], F32)) for i in range(2)]
        pt = [ctx.enter_context(nc.psum_tensor(f"pt{i}", [P, 512], F32)) for i in range(2)]
        pv = [ctx.enter_context(nc.psum_tensor(f"pv{i}", [P, 512], F32)) for i in range(2)]
        pj = ctx.enter_context(nc.psum_tensor("pj", [P, 512], F32))
        po = ctx.enter_context(nc.psum_tensor("po", [P, 512], F32))

        def f(ap):
            return ap.bitcast(F32)

        x_in = sem("x_in")
        par_in = sem("par_in")
        stg_in = sem("stg_in")
        w_hi = sem("w_hi")
        w_lo = sem("w_lo")
        setup_g = sem("setup_g")
        setup_v = sem("setup_v")
        met = sem("met")
        ln_st = sem("ln_st")
        ln_mv = sem("ln_mv")
        ln_ve = sem("ln_ve")
        ln_rs = sem("ln_rs")
        ln_nm = sem("ln_nm")
        ln_hT = sem("ln_hT")
        xb = sem("xb")
        pj_full = sem("pj_full")
        pj_hi = sem("pj_hi")
        pj_free = sem("pj_free")
        v_full = sem("v_full")
        v_hi = sem("v_hi")
        v_free = sem("v_free")
        zeroed = sem("zeroed")
        ctx_in = sem("ctx_in")
        ctx_b = sem("ctx_b")
        a_sc = sem("a_sc")
        a_mx = sem("a_mx")
        a_nb = sem("a_nb")
        a_ex = sem("a_ex")
        a_rc = sem("a_rc")
        a_nm = sem("a_nm")
        a_tp = sem("a_tp")
        a_ph = sem("a_ph")
        a_pl = sem("a_pl")
        a_pv = sem("a_pv")
        a_pc = sem("a_pc")
        a_ot = sem("a_ot")
        a_oh = sem("a_oh")
        a_ol = sem("a_ol")
        a_op = sem("a_op")
        a_xr = sem("a_xr")
        b_sc = sem("b_sc")
        b_mx = sem("b_mx")
        b_nb = sem("b_nb")
        b_ex = sem("b_ex")
        b_rc = sem("b_rc")
        b_nm = sem("b_nm")
        b_tp = sem("b_tp")
        b_ph = sem("b_ph")
        b_pl = sem("b_pl")
        b_pv = sem("b_pv")
        b_pc = sem("b_pc")
        b_ot = sem("b_ot")
        b_oh = sem("b_oh")
        b_ol = sem("b_ol")
        b_op = sem("b_op")
        b_xr = sem("b_xr")
        c_f1 = sem("c_f1")
        c_gl = sem("c_gl")
        c_gh = sem("c_gh")
        c_gw = sem("c_gw")
        c_f2 = sem("c_f2")
        c_xr = sem("c_xr")
        f_ms = sem("f_ms")
        f_mb0 = sem("f_mb0")
        f_ab = sem("f_ab")
        f_ah = sem("f_ah")
        f_al = sem("f_al")
        f_sc = sem("f_sc")
        f_mb = sem("f_mb")
        f_mx = sem("f_mx")
        f_nb = sem("f_nb")
        f_ex = sem("f_ex")
        f_rc = sem("f_rc")
        f_nm = sem("f_nm")
        f_tp = sem("f_tp")
        f_ph = sem("f_ph")
        f_pl = sem("f_pl")
        f_op = sem("f_op")
        f_xr = sem("f_xr")
        f_xc = sem("f_xc")
        f_tt = sem("f_tt")
        f_th = sem("f_th")
        f_tl = sem("f_tl")
        f_st = sem("f_st")
        f_xn = sem("f_xn")
        f_y = sem("f_y")
        out_done = sem("out_done")
        f_in = [sem(f"f_in{i}") for i in range(2)]

        GIVEN = 1

        def barrier(eng, k):
            eng.drain().then_inc(met, 1)
            eng.wait_ge(met, 4 * k)

        def mm3(pe, o, w, m, start, stop, lint=False):
            (wh, wl), (mh, ml) = w, m
            pe.matmul(o, wh, mh, start=start, stop=False, skip_group_check=lint)
            pe.matmul(o, wh, ml, start=False, stop=False, skip_group_check=lint)
            return pe.matmul(o, wl, mh, start=False, stop=stop, skip_group_check=lint)

        def cols(pair, a, b):
            return pair[0][:, a:b], pair[1][:, a:b]

        W0, W1 = (w0h, w0l), (w1h, w1l)

        class At:

            def __init__(self, eng, l, b, ln_stage):
                keep = (lambda v: v if isinstance(v, int) else eng.snap(v))
                self.b = b
                self.t = keep(l * B + b)
                self.heads = keep(self.t * H)
                self.pairs = keep(self.t * NPAIR)
                base, each = ((PRE, USES), (A_USES + 1, NPAIR), (A_USES + B_USES + 1, 1))[ln_stage]
                self.uses = keep(l * LAYER_USES + b * each + base)
                self.lns = keep(l * 27 + b + ln_stage * 9)
                self.biases = keep(l * 24 + 8 * ln_stage + b)
                if ln_stage == 1:
                    self.pairs2 = keep(self.t * H)
                    self.vuses = keep(l * (V_USES * B + 1) + b * V_USES + 1)
                    self.contexts = keep(l * (B + 1) + b)

        def xs(b):
            if isinstance(b, int):
                return xres[:, b, :, :]
            return xres[:, bass.ds(b, 1), :, :].rearrange("p o q c -> p (o q) c")

        def ln_stats(dve, b, n):
            for q in range(2):
                last = dve.bn_stats(stats[:, q, :], xs(b)[:, q, :])
            last.then_inc(ln_st, 1)
            dve.wait_ge(ln_st, n + 1)
            dve.memset(pace[:, :], 0.0)
            for q in range(2):
                last = dve.bn_aggr(mv[:, q, :], stats[:, q, :])
            last.then_inc(ln_mv, 1)

        def ln_rstd(pool, n):
            pool.wait_ge(ln_mv, n + 1)
            pool.tensor_tensor(vare[:, :], mv[:, :, 1], eps[:, :].to_broadcast([P, 2]), ALU.add).then_inc(ln_ve, 1)
            pool.wait_ge(ln_ve, n + 1)
            pool.tensor_tensor(rstd[:, :], vare[:, :], half[:, :], ALU.pow).then_inc(ln_rs, 1)

        def ln_apply(dve, b, n):
            dve.wait_ge(ln_rs, n + 1)
            dve.wait_ge(ln_hT, n + GIVEN)
            for q in range(2):
                last = dve.tensor_scalar(norm[:, q, :], xs(b)[:, q, :], mv[:, q, 0:1], rstd[:, q:q + 1],
                                         ALU.subtract, ALU.mult)
            last.then_inc(ln_nm, 1)

        def ln_turn(pe, use, n, bank=pj, full=pj_full, free=pj_free):
            pe.wait_ge(ln_nm, n + 1)
            pe.wait_ge(free, use - 1 + GIVEN)
            for c in range(2):
                for q in range(2):
                    last = pe.transpose(bank[:, c * S + q * P:c * S + (q + 1) * P],
                                        norm[:, q, c * P:(c + 1) * P], ident[:, :])
            last.then_inc(full, 1)

        def ln_raw(dve, st, use, bank=pj, full=pj_full, free=pj_free):
            dve.wait_ge(full, use)
            for c in range(2):
                g, bb = st * 4 + c, st * 4 + 2 + c
                last = dve.tensor_scalar(htr[:, c, :], bank[:, c * S:(c + 1) * S], pk[:, g:g + 1],
                                         pk[:, bb:bb + 1], ALU.mult, ALU.add)
            last.then_inc(free, 1)

        def ln_hi(act, use):
            act.wait_ge(pj_free, use + GIVEN)
            act.activation(hTh[:, :, :], htr[:, :, :], ACT.Copy).then_inc(pj_hi, 1)

        def ln_lo(pool, use):
            pool.wait_ge(pj_hi, use)
            pool.tensor_tensor(hTl[:, :, :], htr[:, :, :], f(hTh[:, :, :]), ALU.subtract)\
                .then_inc(ln_hT, 1)

        def split_chunk(pool, reg, dst, k):
            pool.wait_ge(stg_in, k * 16)
            if isinstance(dst, int):
                hi, lo = reg[0][:, dst:dst + CH], reg[1][:, dst:dst + CH]
            else:
                hi, lo = reg[0][:, bass.ds(dst, CH)], reg[1][:, bass.ds(dst, CH)]
            pool.tensor_tensor(hi, staged[:, :], ones[:, :].to_broadcast([P, CH]), ALU.mult).then_inc(w_hi, 2)
            pool.wait_ge(w_hi, 2 * k)
            pool.tensor_tensor(lo, staged[:, :], f(hi), ALU.subtract).then_inc(w_lo, 1)

        def split_half(pool, reg, dst, before, i):
            n, half_ = before + i // 2, i % 2
            if half_ == 0:
                pool.wait_ge(stg_in, (n + 1) * 16)
            src = staged[:, half_ * 512:(half_ + 1) * 512]
            if isinstance(dst, int):
                hi, lo = (w[:, dst + half_ * 512:dst + half_ * 512 + 512] for w in reg)
            else:
                hi, lo = (w[:, bass.ds(dst + half_ * 512, 512)] for w in reg)
            pool.tensor_tensor(hi, src, ones[:, :].to_broadcast([P, 512]), ALU.mult).then_inc(w_hi, 1)
            pool.wait_ge(w_hi, n * 2 + half_ + 1)
            last = pool.tensor_tensor(lo, src, f(hi), ALU.subtract)
            if half_:
                last.then_inc(w_lo, 1)

        def use_at(a, what):
            if what in (("ln", 0), ("qk", 0), ("v", 0)):
                return a.uses - PRE + {"ln": 1, "qk": 2, "v": 3}[what[0]]
            return a.uses + A_OF[what] + 1

        def new_use(a, h):
            return a.uses + A_NTH[h] + 1

        def pe_proj(pe, a, what, use, ln):
            kind, i = what
            if kind == "ln":
                ln_turn(pe, use, ln)
                return
            pe.wait_ge(pj_free, use - 1 + GIVEN)
            pe.wait_ge(ln_hT, ln + GIVEN)
            if kind == "qk":
                at = QK_AT[i // 2] + (i % 2) * 512
                for qk in range(2):
                    for c in range(2):
                        w = at + qk * 256 + c * P
                        last = mm3(pe, pj[:, qk * S:(qk + 1) * S], cols(W0, w, w + P),
                                   (hTh[:, c, :], hTl[:, c, :]), c == 0, c == 1)
            else:
                for kt in range(2):
                    for c in range(2):
                        w = V_AT[i] + c * 256
                        last = mm3(pe, pj[:, kt * 256:(kt + 1) * 256],
                                   (hTh[:, c, kt * P:(kt + 1) * P], hTl[:, c, kt * P:(kt + 1) * P]),
                                   cols(W0, w, w + 256), c == 0, c == 1)
            last.then_inc(pj_full, 1)

        def act_proj(act, a, what, use, reader):
            kind, i = what
            if kind == "ln":
                ln_hi(act, use)
                return
            act.wait_ge(pj_full, use)
            if reader:
                act.wait_ge(*reader)
            if kind == "qk":
                o, i_ = qkh[:, i % 2, :], pj[:, :]
            else:
                o = vhl[:, i % 2, :, :, 0:D]
                i_ = pj[:, :].rearrange("p (k h d) -> p k h d", k=2, h=4)
            act.activation(o, i_, ACT.Copy).then_inc(pj_hi, 1)

        def dve_proj(dve, a, what, use, st=0):
            kind, i = what
            if kind == "ln":
                ln_raw(dve, st, use)
                return
            dve.wait_ge(pj_hi, use)
            if kind == "qk":
                o, i_, h_ = qkl[:, i % 2, :], pj[:, :], qkh[:, i % 2, :]
            else:
                o, h_ = vhl[:, i % 2, :, :, D:2 * D], vhl[:, i % 2, :, :, 0:D]
                i_ = pj[:, :].rearrange("p (k h d) -> p k h d", k=2, h=4)
            dve.tensor_tensor(o, i_, f(h_), ALU.subtract).then_inc(pj_free, 1)

        def a_slot_pe(pe, a, h, mode):
            new, old = mode != "tail", (lambda k: h - k >= 0 or mode != "first")
            N = lambda k: a.heads + (h - k) + 1
            if old(2) and (new or h - 2 < 0):
                m = h % 2
                pe.wait_ge(a_nm, N(2))
                if old(4):
                    pe.wait_ge(a_pl, N(4))
                for kt in range(2):
                    for q in range(2):
                        last = pe.transpose(pt[m][:, kt * S + q * P:kt * S + (q + 1) * P],
                                            prob[:, m, q * S + kt * P:q * S + (kt + 1) * P], ident[:, :])
                last.then_inc(a_tp, 1)
            if new:
                p, j = h // 2, h % 2
                pe.wait_ge(pj_free, use_at(a, ("qk", p)) + GIVEN)
                if old(2):
                    pe.wait_ge(a_ex, N(2))
                r = slice(D * j, D * j + D)
                for q in range(2):
                    qs = slice(q * P, (q + 1) * P)
                    last = mm3(pe, sc[h % 2][:, q * S:(q + 1) * S],
                               (qkh[r, p % 2, qs], qkl[r, p % 2, qs]),
                               (qkh[r, p % 2, S:2 * S], qkl[r, p % 2, S:2 * S]), True, True)
                last.then_inc(a_sc, 1)
            if old(3) and (new or h - 3 < 0):
                hh = (h - 3) % H
                m = hh % 2
                pe.wait_ge(a_pl, N(3))
                pe.wait_ge(pj_free, use_at(a, ("v", hh // 4)) - (USES if h < 3 else 0) + GIVEN)
                if old(5):
                    pe.wait_ge(a_ot, N(5))
                for kt in range(2):
                    v = vhl[:, (hh // 4) % 2, kt, hh % 4, :]
                    pe.matmul(pv[m][:, 0:S], v, pth[:, m, kt * S:(kt + 1) * S], start=kt == 0, stop=False)
                    last = pe.matmul(pv[m][:, 0:S], v, ptl[:, m, kt * S:(kt + 1) * S], start=False,
                                     stop=kt == 1)
                last.then_inc(a_pv, 1)
            if h % 2 == 0 and old(6) and (new or h - 6 < 0):
                p = ((h - 6) // 2) % NPAIR
                pe.wait_ge(a_ol, a.pairs + (h - 6) // 2 + 1)
                if p == 0 and mode != "first":
                    pe.wait_ge(a_xr, a.t)
                for q in range(2):
                    qs = slice(q * P, (q + 1) * P)
                    w = O_AT + p * 256
                    last = mm3(pe, po[:, q * C:(q + 1) * C], (oth[:, p % 2, qs], otl[:, p % 2, qs]),
                               cols(W0, w, w + 256), p == 0 and q == 0, p == NPAIR - 1, lint=True)
                last.then_inc(a_op, 1)
            if new and h in A_USE:
                what = A_USE[h]
                pe_proj(pe, a, what, new_use(a, h), a.lns + (2 if h >= 14 else 1))

        def a_slot_act(act, a, h, mode):
            new, old = mode != "tail", (lambda k: h - k >= 0 or mode != "first")
            N = lambda k: a.heads + (h - k) + 1
            if old(2) and (new or h - 2 < 0):
                m = h % 2
                act.wait_ge(a_tp, N(2))
                if old(4):
                    act.wait_ge(a_pv, N(4))
                act.activation(pth[:, m, :], pt[m][:, :], ACT.Copy).then_inc(a_ph, 1)
            if old(3) and (new or h - 3 < 0):
                j = (h - 3) % 2
                act.wait_ge(a_pv, N(3))
                if old(5):
                    act.wait_ge(a_ot, N(5))
                src, dst = (slice(D, P), slice(0, D)) if j == 0 else (slice(0, D), slice(D, P))
                act.activation(part[dst, :], pv[j][src, 0:S], ACT.Copy).then_inc(a_pc, 1)
            if new:
                m = h % 2
                act.wait_ge(a_nb, N(0))
                if old(2):
                    act.wait_ge(a_tp, N(2))
                for q in range(2):
                    last = act.activation(prob[:, m, q * S:(q + 1) * S], sc[m][:, q * S:(q + 1) * S], ACT.Exp,
                                          bias=nbias[:, m, q:q + 1], scale=SCALE,
                                          accum_out=psums[:, m, q:q + 1])
                last.then_inc(a_ex, 1)
            if new and h in A_USE:
                what = A_USE[h]
                reader = None
                if what[0] == "qk" and (h >= 1 or mode != "first"):
                    reader = (a_sc, a.heads + h)
                if what[0] == "v" and (h > 3 or mode != "first"):
                    reader = (a_pv, a.heads + h - 3)
                act_proj(act, a, what, new_use(a, h), reader)

        def a_slot_dve(dve, a, h, mode, b):
            new, old = mode != "tail", (lambda k: h - k >= 0 or mode != "first")
            N = lambda k: a.heads + (h - k) + 1
            m = h % 2
            if old(1) and (new or h - 1 < 0):
                n = (h - 1) % 2
                dve.wait_ge(a_ex, N(1))
                dve.reciprocal(rsum[:, n, 0:2], psums[:, n, 0:2]).then_inc(a_rc, 1)
            if new:
                dve.wait_ge(a_sc, N(0))
                dve.tensor_reduce(nmax[:, m, 0:2], sc[m][:, :].rearrange("p (q k) -> p q k", q=2), AX.X, ALU.max,
                                  negate=True).then_inc(a_mx, 1)
                dve.wait_ge(a_mx, N(0))
                dve.tensor_scalar(nbias[:, m, 0:2], nmax[:, m, 0:2], SCALE, None, ALU.mult)\
                    .then_inc(a_nb, 1)
            if old(2) and (new or h - 2 < 0):
                dve.wait_ge(a_ph, N(2))
                dve.tensor_tensor(ptl[:, m, :], pt[m][:, :], f(pth[:, m, :]), ALU.subtract)\
                    .then_inc(a_pl, 1)
            if old(3) and (new or h - 3 < 0):
                hh = (h - 3) % H
                p, j = hh // 2, hh % 2
                dve.wait_ge(a_pc, N(3))
                if j == 0 and old(7):
                    dve.wait_ge(a_ol, a.pairs + (h - 3) // 2 - 1)
                r = slice(D * j, D * j + D)
                dve.tensor_tensor(otr[r, p % 2, :], pv[j][r, 0:S], part[r, :], ALU.add).then_inc(a_ot, 1)
            if h == 5 and mode != "first":
                residual(dve, a_op, a.pairs, a_xr, b - 1, a.biases)
            if new and h in A_USE:
                dve_proj(dve, a, A_USE[h], new_use(a, h))
            if new and h == 7:
                ln_stats(dve, b + 1, a.lns + 1)
            if new and h == 9:
                ln_apply(dve, b + 1, a.lns + 1)

        def residual(dve, full, count, done, b, xbs):
            dve.wait_ge(full, count)
            dve.wait_ge(xb, xbs)
            dve.tensor_tensor(xs(b), po[:, :].rearrange("p (q c) -> p q c", q=2), xs(b), ALU.add)\
                .then_inc(done, 1)

        def add_bias(pool, b, st):
            bias = brow[:, st:st + 1, :].to_broadcast([P, 2, C])
            pool.tensor_tensor(xs(b), xs(b), bias, ALU.add).then_inc(xb, 1)

        def pair_split(pool, out_sem, count_out, hi_sem, lo_sem, count, m):
            pool.wait_ge(out_sem, count_out)
            pool.tensor_tensor(oth[:, m, :], otr[:, m, :], ones[:, :].to_broadcast([P, S]), ALU.mult)\
                .then_inc(hi_sem, 1)
            pool.wait_ge(hi_sem, count)
            pool.tensor_tensor(otl[:, m, :], otr[:, m, :], f(oth[:, m, :]), ALU.subtract)\
                .then_inc(lo_sem, 1)

        def a_slot_pool(pool, a, h, mode, b, l):
            new, old = mode != "tail", (lambda k: h - k >= 0 or mode != "first")
            N = lambda k: a.heads + (h - k) + 1
            if old(1) and (new or h - 1 < 0):
                v = prob[:, (h - 1) % 2, :].rearrange("p (q k) -> p q k", q=2)
                pool.wait_ge(a_rc, N(1))
                pool.tensor_tensor(v, v, rsum[:, (h - 1) % 2, 0:2].unsqueeze(2).to_broadcast([P, 2, S]),
                                   ALU.mult).then_inc(a_nm, 1)
            if h % 2 == 0 and old(4) and (new or h - 4 < 0):
                g = a.pairs + (h - 4) // 2
                if old(8):
                    pool.wait_ge(a_op, g - 1)
                pair_split(pool, a_ot, N(3), a_oh, a_ol, g + 1, ((h - 4) // 2) % 2)
            if new and mode == "first" and h < 8:
                split_half(pool, W0, LOW_ORDER[h // 2] * CH, l * PER_LAYER + NA_HIGH, h)
            if new and h in (9, 11):
                split_half(pool, W1, b * CH, l * PER_LAYER + b + NA_HIGH + NA_LOW, h // 11)
            if new and h == 8:
                ln_rstd(pool, a.lns + 1)
            if new and h == 12:
                pool.wait_ge(ln_nm, a.lns + 1)
                add_bias(pool, b, 0)
            if new and h == 13:
                ln_lo(pool, new_use(a, 13))

        BQ, BK, BV, BO = 0, 2 * CH, 4 * CH, 6 * CH

        vb = pv[1]
        kbk = vhl[:, :, 1, :, :].rearrange("p m h d -> p m (h d)")

        def ctxs(t, e, b, n):
            if isinstance(b, int):
                return t[:, e, b * KP:b * KP + n]
            return t[:, e, bass.ds(b * KP, n)]

        cbh = qkh[:, :, S:S + KP]
        cbl = qkl[:, :, S:S + KP]

        def b_qk_pe(pe, i, use, ln, ctx_b):
            pe.wait_ge(pj_free, use - 1 + GIVEN)
            pe.wait_ge(ln_hT, ln + GIVEN)
            for c in range(2):
                w = BQ + i * 256 + c * P
                mm3(pe, pj[:, 0:S], cols(W1, w, w + P), (hTh[:, c, :], hTl[:, c, :]), c == 0, c == 1)
            for e in range(2):
                w = BK + i * 256 + e * P
                last = mm3(pe, pj[:, S:S + KP], cols(W1, w, w + P),
                           (ctxs(cTh, e, ctx_b, KP), ctxs(cTl, e, ctx_b, KP)), e == 0, e == 1)
            last.then_inc(pj_full, 1)

        def b_qk_act(act, i, use):
            act.wait_ge(pj_full, use)
            m = i % 2
            act.activation(qkh[:, m, 0:S], pj[:, 0:S], ACT.Copy)
            for j in range(2):
                r = slice(D * j, D * j + D)
                last = act.activation(kbk[r, m, j * KP:(j + 1) * KP], pj[r, S:S + KP], ACT.Copy)
            last.then_inc(pj_hi, 1)

        def b_qk_dve(dve, i, use):
            dve.wait_ge(pj_hi, use)
            m = i % 2
            dve.tensor_tensor(qkl[:, m, 0:S], pj[:, 0:S], f(qkh[:, m, 0:S]), ALU.subtract)
            for j in range(2):
                r = slice(D * j, D * j + D)
                last = dve.tensor_tensor(kbk[r, m, 2 * KP + j * KP:2 * KP + (j + 1) * KP],
                                         pj[r, S:S + KP], f(kbk[r, m, j * KP:(j + 1) * KP]), ALU.subtract)
            last.then_inc(pj_free, 1)

        def b_v_pe(pe, i, use):
            pe.wait_ge(v_free, use - 1 + GIVEN)
            for e in range(2):
                w = BV + i * 512 + e * 256
                last = mm3(pe, vb[0:KC, 0:256], (cbh[:, e, 0:KC], cbl[:, e, 0:KC]), cols(W1, w, w + 256),
                           e == 0, e == 1)
            last.then_inc(v_full, 1)

        def b_v_act(act, i, use):
            act.wait_ge(v_full, use)
            act.activation(vhl[0:KC, i % 2, 0, :, 0:D], vb[0:KC, 0:256].rearrange("p (h d) -> p h d", h=4),
                           ACT.Copy).then_inc(v_hi, 1)

        def b_v_dve(dve, i, use):
            dve.wait_ge(v_hi, use)
            dve.tensor_tensor(vhl[0:KC, i % 2, 0, :, D:2 * D],
                              vb[0:KC, 0:256].rearrange("p (h d) -> p h d", h=4),
                              f(vhl[0:KC, i % 2, 0, :, 0:D]), ALU.subtract).then_inc(v_free, 1)

        def b_ln_hi(act, use):
            act.wait_ge(v_free, use + GIVEN)
            act.activation(hTh[:, :, :], htr[:, :, :], ACT.Copy).then_inc(v_hi, 1)

        def b_ln_lo(dve, use):
            dve.wait_ge(v_hi, use)
            dve.tensor_tensor(hTl[:, :, :], htr[:, :, :], f(hTh[:, :, :]), ALU.subtract).then_inc(ln_hT, 1)

        def b_slot_pe(pe, a, p, mode, b):
            new, old = mode != "tail", (lambda k: p - k >= 0 or mode != "first")
            N = lambda k: a.pairs + (p - k) + 1
            if old(2) and (new or p - 2 < 0):
                m = p % 2
                pe.wait_ge(b_nm, N(2))
                if old(4):
                    pe.wait_ge(b_pl, N(4))
                for j in range(2):
                    for q in range(2):
                        last = pe.transpose(pt[m][0:KC, j * S + q * P:j * S + (q + 1) * P],
                                            prob[:, m, (q * 2 + j) * KC:(q * 2 + j + 1) * KC], ident[:, :])
                last.then_inc(b_tp, 1)
            if new:
                m = p % 2
                pe.wait_ge(pj_free, a.uses + p + GIVEN)
                if old(2):
                    pe.wait_ge(b_ex, N(2))
                for q in range(2):
                    qs = slice(q * P, (q + 1) * P)
                    last = mm3(pe, sc[m][:, q * 2 * KP:(q + 1) * 2 * KP], (qkh[:, m, qs], qkl[:, m, qs]),
                               (kbk[:, m, 0:2 * KP], kbk[:, m, 2 * KP:4 * KP]), True, True)
                last.then_inc(b_sc, 1)
                nxt = p == 7
                b_qk_pe(pe, (p + 1) % NPAIR, a.uses + p + 1, a.lns + (2 if nxt else 1), b + 1 if nxt else b)
            if old(3) and (new or p - 3 < 0):
                pp = (p - 3) % NPAIR
                m = pp % 2
                pe.wait_ge(b_pl, N(3))
                pe.wait_ge(v_free, a.vuses + V_OF[pp // 2] - (V_USES if p < 3 else 0) + GIVEN)
                if old(4):
                    pe.wait_ge(b_ot, a.pairs2 + (p - 4) * 2 + 2)
                for j in range(2):
                    v = vhl[0:KC, (pp // 2) % 2, 0, (pp % 2) * 2 + j, :]
                    o = pv[0][:, j * S:(j + 1) * S]
                    pe.matmul(o, v, pth[0:KC, m, j * S:(j + 1) * S], start=True, stop=False)
                    last = pe.matmul(o, v, ptl[0:KC, m, j * S:(j + 1) * S], start=False, stop=True)
                last.then_inc(b_pv, 1)
            if new and p % 2 == 0:
                if p == 0:
                    pe.wait_ge(ctx_b, a.contexts + 1)
                b_v_pe(pe, p // 2, a.vuses + V_OF[p // 2])
            if new and p == 5:
                ln_turn(pe, a.vuses + 4, a.lns + 1, vb, v_full, v_free)
            if old(5) and (new or p - 5 < 0):
                pp = (p - 5) % NPAIR
                pe.wait_ge(b_ol, N(5))
                if pp == 0 and mode != "first":
                    pe.wait_ge(b_xr, a.t)
                for q in range(2):
                    qs = slice(q * P, (q + 1) * P)
                    w = BO + pp * 256
                    last = mm3(pe, po[:, q * C:(q + 1) * C], (oth[:, pp % 2, qs], otl[:, pp % 2, qs]),
                               cols(W1, w, w + 256), pp == 0 and q == 0, pp == NPAIR - 1, lint=True)
                last.then_inc(b_op, 1)

        def b_slot_act(act, a, p, mode):
            new, old = mode != "tail", (lambda k: p - k >= 0 or mode != "first")
            N = lambda k: a.pairs + (p - k) + 1
            if old(2) and (new or p - 2 < 0):
                m = p % 2
                act.wait_ge(b_tp, N(2))
                if old(4):
                    act.wait_ge(b_pv, N(4))
                act.activation(pth[0:KC, m, :], pt[m][0:KC, :], ACT.Copy).then_inc(b_ph, 1)
            if new:
                m = p % 2
                act.wait_ge(b_nb, N(0))
                if old(2):
                    act.wait_ge(b_tp, N(2))
                for k in range(4):
                    q, j = k // 2, k % 2
                    last = act.activation(prob[:, m, k * KC:(k + 1) * KC],
                                          sc[m][:, q * 2 * KP + j * KP:q * 2 * KP + j * KP + KC], ACT.Exp,
                                          bias=nbias[:, m, k:k + 1], scale=SCALE,
                                          accum_out=psums[:, m, k:k + 1])
                last.then_inc(b_ex, 1)
                if p >= 1 or mode != "first":
                    act.wait_ge(b_sc, a.pairs + p)
                b_qk_act(act, (p + 1) % NPAIR, a.uses + p + 1)
                if p == 6:
                    b_ln_hi(act, a.vuses + 4)
            if old(3) and (new or p - 3 < 0):
                act.wait_ge(b_pv, N(3))
                if old(4):
                    act.wait_ge(b_ot, a.pairs2 + (p - 4) * 2 + 2)
                for j in range(2):
                    src, dst = (slice(D, P), slice(0, D)) if j == 0 else (slice(0, D), slice(D, P))
                    last = act.activation(part[dst, :], pv[0][src, j * S:(j + 1) * S], ACT.Copy)
                last.then_inc(b_pc, 1)
            if new and p % 2 == 0:
                if old(3):
                    act.wait_ge(b_pv, N(3))
                b_v_act(act, p // 2, a.vuses + V_OF[p // 2])

        def b_slot_dve(dve, a, p, mode, b):
            new, old = mode != "tail", (lambda k: p - k >= 0 or mode != "first")
            N = lambda k: a.pairs + (p - k) + 1
            m = p % 2
            if old(1) and (new or p - 1 < 0):
                n = (p - 1) % 2
                dve.wait_ge(b_ex, N(1))
                dve.reciprocal(rsum[:, n, :], psums[:, n, :]).then_inc(b_rc, 1)
            if old(4) and (new or p - 4 < 0):
                dve.wait_ge(b_pc, N(4))
                if old(6):
                    dve.wait_ge(b_ol, N(6))
                for j in range(2):
                    r = slice(D * j, D * j + D)
                    dve.tensor_tensor(otr[r, m, :], pv[0][r, j * S:(j + 1) * S], part[r, :], ALU.add)\
                        .then_inc(b_ot, 1)
            if p == 5 and mode != "first":
                residual(dve, b_op, a.pairs, b_xr, b - 1, a.biases)
            if new:
                dve.wait_ge(b_sc, N(0))
                dve.tensor_reduce(nmax[:, m, :], sc[m][:, 0:4 * KP].rearrange("p (g k) -> p g k", g=4)[:, :, 0:KC],
                                  AX.X, ALU.max, negate=True).then_inc(b_mx, 1)
                dve.wait_ge(b_mx, N(0))
                dve.tensor_scalar(nbias[:, m, :], nmax[:, m, :], SCALE, None, ALU.mult).then_inc(b_nb, 1)
            if old(2) and (new or p - 2 < 0):
                dve.wait_ge(b_ph, N(2))
                dve.tensor_tensor(ptl[0:KC, m, :], pt[m][0:KC, :], f(pth[0:KC, m, :]), ALU.subtract)\
                    .then_inc(b_pl, 1)
            if new:
                if p % 2 == 1:
                    b_v_dve(dve, p // 2, a.vuses + V_OF[p // 2])
                if p == 1:
                    ln_stats(dve, b + 1, a.lns + 1)
                if p == 3:
                    ln_apply(dve, b + 1, a.lns + 1)
                if p == 6:
                    ln_raw(dve, 1, a.vuses + 4, vb, v_full, v_free)
                if p == 7:
                    context_to_fixed(dve, b + 1, v_free, a.vuses + V_USES + GIVEN)
                b_qk_dve(dve, (p + 1) % NPAIR, a.uses + p + 1)
                if p == 6:
                    b_ln_lo(dve, a.vuses + 4)

        def context_to_fixed(dve, b, free, value):
            dve.wait_ge(free, value)
            for src, dst in ((cTh, cbh), (cTl, cbl)):
                last = dve.tensor_copy(dst, f(src[:, :, b * KP:(b + 1) * KP]) if isinstance(b, int)
                                       else f(src[:, :, bass.ds(b * KP, KP)]))
            last.then_inc(ctx_b, 1)

        def b_slot_pool(pool, a, p, mode, b, l):
            new, old = mode != "tail", (lambda k: p - k >= 0 or mode != "first")
            N = lambda k: a.pairs + (p - k) + 1
            if old(1) and (new or p - 1 < 0):
                n = (p - 1) % 2
                pool.wait_ge(b_rc, N(1))
                v = prob[:, n, 0:4 * KC].rearrange("p (g k) -> p g k", g=4)
                pool.tensor_tensor(v, v, rsum[:, n, :].unsqueeze(2).to_broadcast([P, 4, KC]), ALU.mult)\
                    .then_inc(b_nm, 1)
            if old(4) and (new or p - 4 < 0):
                if old(6):
                    pool.wait_ge(b_op, N(6))
                pair_split(pool, b_ot, a.pairs2 + (p - 4) * 2 + 2, b_oh, b_ol, N(4), p % 2)
            if new and p in (0, 4):
                split_half(pool, W0, b * CH, l * PER_LAYER + b + NA_HIGH + NA_LOW + NB, p // 4)
            if new and p == 2:
                ln_rstd(pool, a.lns + 1)
            if new and p == 5:
                pool.wait_ge(ln_nm, a.lns + 1)
                add_bias(pool, b, 1)

        g_raw = [prob[:, 0, 0:S], prob[:, 0, S:2 * S], prob[:, 1, 0:S], prob[:, 1, S:2 * S]]
        g_hi = [pth[:, i // 2, (i % 2) * S:(i % 2 + 1) * S] for i in range(4)]
        g_lo = [ptl[:, i // 2, (i % 2) * S:(i % 2 + 1) * S] for i in range(4)]
        f1 = [sc[0], sc[1], pt[0], pt[1]]

        def c_slot_pe(pe, a, m, mode):
            new, old = mode != "tail", (lambda k: m - k >= 0 or mode != "first")
            N = lambda k: a.pairs + (m - k) + 1
            if old(2) and (new or m - 2 < 0):
                mm_, i = (m - 2) % 8, (m - 2) % 4
                pe.wait_ge(c_gw, N(2))
                if mm_ == 0 and mode != "first":
                    pe.wait_ge(c_xr, a.t)
                for q in range(2):
                    w = 2 * CH + mm_ * 256
                    last = mm3(pe, po[:, q * C:(q + 1) * C],
                               (g_hi[i][:, q * P:(q + 1) * P], g_lo[i][:, q * P:(q + 1) * P]),
                               cols(W0, w, w + 256), mm_ == 0 and q == 0, mm_ == 7, lint=True)
                last.then_inc(c_f2, 1)
            if new:
                pe.wait_ge(ln_hT, a.lns + 1 + GIVEN)
                if old(4):
                    pe.wait_ge(c_gl, N(4))
                for c in range(2):
                    w = m * 256 + c * P
                    last = mm3(pe, f1[m % 4][:, 0:S], cols(W0, w, w + P), (hTh[:, c, :], hTl[:, c, :]),
                               c == 0, c == 1)
                last.then_inc(c_f1, 1)
                if m == 7:
                    ln_turn(pe, a.uses + 1, a.lns + 1)

        def c_slot_act(act, a, m, mode):
            N = lambda k: a.pairs + (m - k) + 1
            act.wait_ge(c_f1, N(0))
            if m >= 4 or mode != "first":
                act.wait_ge(c_gw, N(4))
            act.activation(g_raw[m % 4], f1[m % 4][:, 0:S], ACT.Gelu, bias=pk[:, 12 + m:13 + m])\
                .then_inc(c_gl, 1)
            if m == 7:
                ln_hi(act, a.uses + 1)

        def c_slot_dve(dve, a, m, mode, b):
            new = mode != "tail"
            N = lambda k: a.pairs + (m - k) + 1
            if m == 2 and mode != "first":
                residual(dve, c_f2, a.pairs, c_xr, b - 1, a.biases)
            if new:
                dve.wait_ge(c_gl, N(0))
                if m >= 4 or mode != "first":
                    dve.wait_ge(c_f2, N(4))
                dve.tensor_copy(g_hi[m % 4], g_raw[m % 4]).then_inc(c_gh, 1)
            if new:
                if m == 3:
                    ln_stats(dve, b + 1, a.lns + 1)
                if m == 5:
                    ln_apply(dve, b + 1, a.lns + 1)
                if m == 7:
                    ln_raw(dve, 2, a.uses + 1)

        def c_slot_pool(pool, a, m, mode, b):
            N = lambda k: a.pairs + (m - k) + 1
            pool.wait_ge(c_gh, N(0))
            pool.tensor_tensor(g_lo[m % 4], g_raw[m % 4], f(g_hi[m % 4]), ALU.subtract).then_inc(c_gw, 1)
            if m == 4:
                ln_rstd(pool, a.lns + 1)
            if m == 6:
                pool.wait_ge(ln_nm, a.lns + 1)
                add_bias(pool, b, 2)
            if m == 7:
                ln_lo(pool, a.uses + 1)

        def run(eng, stage, l, bar, pre, slot, slots, tails):
            def at(b):
                return At(eng, l, b, stage)
            a = at(0)
            pre(a)
            for i in range(slots):
                slot(a, i, "first", 0)
            with eng.Fori(1, B) as b:
                a = at(b)
                for i in range(slots):
                    slot(a, i, "steady", b)
            a = at(B)
            for i in range(tails):
                slot(a, i, "tail", B)
            barrier(eng, bar)

        ctx_raw0 = prob[:, :, :].rearrange("p m n -> p (m n)")[:, 0:CW]
        ctx_raw1 = brow[:, :, :].rearrange("p m n -> p (m n)")[:, 0:CW]

        KOH, PAIRC = 312, 4 * KC
        END = 3 * L
        G_COLS = HF * KOH
        VO_AT = 2 * G_COLS
        MB = brow[:, :, :].rearrange("p m n -> p (m n)")[:, 0:B * KC]
        GB = xres[:, B, :, :]
        stage2 = [staged[:, :], prob[:, :, :].rearrange("p m n -> p (m n)")]
        yout = otr

        def final_sync(sp):
            for i in range(12):
                k = NSTREAM + i
                if i < 2:
                    sp.wait_ge(met, 4 * END)
                else:
                    sp.wait_ge(w_lo, k - 1)
                sp.dma_start(stage2[i % 2], wts[k, :, :]).then_inc(f_in[i % 2], 16)
            sp.wait_ge(w_lo, NCHUNK)
            sp.dma_start(staged[:, 0:B * KC].bitcast(I32), mask.rearrange("b k -> (b k)").partition_broadcast(P))\
                .then_inc(f_ms, 16)
            sp.dma_start(GB, rows_f.rearrange("r c -> (r c)").partition_broadcast(P)
                         .rearrange("p (r c) -> p r c", r=2)).then_inc(f_ms, 16)

            def store(b):
                sp.wait_ge(f_y, b + 1)
                o = out.rearrange("b (q p) c -> b p q c", p=P)
                o = o[b] if isinstance(b, int) else o[bass.ds(b, 1), :, :, :].rearrange("o p q c -> p (o q) c")
                sp.dma_start(o, yout[:, :, :]).then_inc(out_done, 16)
            with sp.Fori(0, B) as b:
                store(b)
            sp.wait_ge(out_done, 16 * B + 16)

        def unit_evac_act(act, u, n, dst, part_=P):
            m = u[1]
            act.wait_ge(f_ab, u[0] + 1)
            act.activation(dst[0], f1[m][0:part_, 0:n], ACT.Copy).then_inc(f_ah, 1)

        def unit_evac_dve(dve, u, n, dst, part_=P):
            m = u[1]
            dve.wait_ge(f_ah, u[0] + 1)
            dve.tensor_tensor(dst[1], f1[m][0:part_, 0:n], f(dst[0]), ALU.subtract).then_inc(f_al, 1)

        def g_dst(h, c):
            return cols(W0, c * G_COLS + h * KOH, c * G_COLS + (h + 1) * KOH)

        def vo_dst(i):
            return [w[0:KC, VO_AT + i * 512:VO_AT + (i + 1) * 512] for w in W0]

        HALF_UNITS = 16 + 4 * 4

        def final_pe(pe):
            for u in range(16):
                h, second = u % 8, u // 8
                pe.wait_ge(w_lo, NSTREAM + (4 + 2 * (h // 2) + 2 if second else h // 2 + 1))
                if u >= 4:
                    pe.wait_ge(f_al, u - 3)
                for e in range(2):
                    for dc in range(2):
                        w = h * 512 + dc * 256
                        last = mm3(pe, f1[u % 4][:, e * 256:(e + 1) * 256],
                                   cols(W0, w + e * P, w + (e + 1) * P), cols(W0, 4096 + w, 4096 + w + 256),
                                   dc == 0, dc == 1)
                last.then_inc(f_ab, 1)

            def half_(hb):
                base = 16 + HALF_UNITS * hb
                for i in range(16):
                    h, c = i // 2, i % 2
                    pe.wait_ge(f_al, base + i - 3)
                    if i == 0:
                        pe.wait_ge(f_al, base)
                    for e in range(2):
                        w = (h * 2 + e) * 256 + c * P
                        last = mm3(pe, f1[i % 4][:, 0:KOH], cols(W1, w, w + P),
                                   (ctxh(cTh, e, hb), ctxh(cTl, e, hb)), e == 0, e == 1)
                    last.then_inc(f_ab, 1)
                with pe.Fori(0, 4) as b4:
                    batch(hb, b4)

            def ctxh(t, e, hb):
                return t[:, e, hb * KOH:(hb + 1) * KOH]

            def batch(hb, b4):
                t = pe.snap(b4 + hb * 4)
                u0 = pe.snap(t * 4 + 16 + 16 * (hb + 1))
                n4 = pe.snap(t * 4)
                pe.wait_ge(f_xc, t + 1)
                for c in range(2):
                    for q in range(2):
                        last = pe.transpose(pj[:, c * S + q * P:c * S + (q + 1) * P],
                                            norm[:, q, c * P:(c + 1) * P], ident[:, :])
                last.then_inc(f_tt, 1)
                pe.wait_ge(ctx_b, t + L * (B + 1) + 1)
                pe.wait_ge(f_al, u0)
                for i in range(4):
                    for e in range(2):
                        m = [w[:, 4096 + i * 1024:4096 + (i + 1) * 1024].rearrange("p (h e c) -> p h e c", h=2, e=2)
                             [:, :, e, :] for w in W1]
                        last = mm3(pe, f1[i][0:KC, :], (cbh[:, e, 0:KC], cbl[:, e, 0:KC]), m, e == 0, e == 1)
                    last.then_inc(f_ab, 1)
                pe.wait_ge(f_al, u0 + 4)
                pe.wait_ge(f_tl, t + 1)
                for k in range(6):
                    if k < 4:
                        q, hh, m = k // 2, k % 2, k % 2
                        if k >= 2:
                            pe.wait_ge(f_mb, n4 + k - 1)
                        for c in range(2):
                            g = [w[:, c * G_COLS + hh * 4 * KOH:c * G_COLS + (hh + 1) * 4 * KOH]
                                 .rearrange("p (h n) -> p h n", h=4)[:, :, bass.ds(b4 * KP, KP)] for w in W0]
                            last = mm3(pe, sc[m][:, 0:KOH],
                                       (hTh[:, c, q * P:(q + 1) * P], hTl[:, c, q * P:(q + 1) * P]), g,
                                       c == 0, c == 1)
                        last.then_inc(f_sc, 1)
                    if 1 <= k < 5:
                        m = (k - 1) % 2
                        pe.wait_ge(f_nm, n4 + k)
                        for h in range(4):
                            last = pe.transpose(pt[m][0:KC, h * P:(h + 1) * P],
                                                prob[:, m, h * KC:(h + 1) * KC], ident[:, :])
                        last.then_inc(f_tp, 1)
                    if k >= 2:
                        m, q, hh = k % 2, (k - 2) // 2, k % 2
                        pe.wait_ge(f_pl, n4 + k - 1)
                        for h in range(4):
                            w = VO_AT + (hh * 4 + h) * 256
                            last = mm3(pe, po[:, q * C:(q + 1) * C],
                                       (pth[0:KC, m, h * P:(h + 1) * P], ptl[0:KC, m, h * P:(h + 1) * P]),
                                       [x_[0:KC, w:w + 256] for x_ in W0],
                                       k == 2 and h == 0, hh == 1 and h == 3, lint=True)
                        last.then_inc(f_op, 1)
            for hb in range(2):
                half_(hb)

        def final_act(act):
            for u in range(16):
                base = 4096 * (u // 8) + (u % 8) * 512
                unit_evac_act(act, (u, u % 4), 512, cols(W1, base, base + 512))
            for hb in range(2):
                base = 16 + HALF_UNITS * hb
                for i in range(16):
                    if i == 0:
                        act.wait_ge(f_ab, 16)
                        if hb:
                            act.wait_ge(f_op, 16)
                    unit_evac_act(act, (base + i, i % 4), KOH, g_dst(i // 2, i % 2))
                with act.Fori(0, 4) as b4:
                    t = act.snap(b4 + hb * 4)
                    u0 = act.snap(t * 4 + 16 + 16 * (hb + 1))
                    n4 = act.snap(t * 4)
                    act.wait_ge(f_tt, t + 1)
                    act.activation(hTh[:, :, :], pj[:, :].rearrange("p (c n) -> p c n", c=2), ACT.Copy)\
                        .then_inc(f_th, 1)
                    for i in range(4):
                        unit_evac_act(act, (u0 + i, i), 512, vo_dst(i), KC)
                    for k in range(5):
                        if k >= 1:
                            m = (k - 1) % 2
                            act.wait_ge(f_tp, n4 + k)
                            if k >= 3:
                                act.wait_ge(f_op, n4 + k - 2)
                            act.activation(pth[0:KC, m, :], pt[m][0:KC, :], ACT.Copy).then_inc(f_ph, 1)
                        if k < 4:
                            m = k % 2
                            act.wait_ge(f_nb, n4 + k + 1)
                            for h in range(4):
                                v = prob[:, m, h * KC:(h + 1) * KC]
                                last = act.activation(v, v, ACT.Exp, bias=nbias[:, m, h:h + 1], scale=SCALE_F,
                                                      accum_out=psums[:, m, h:h + 1])
                            last.then_inc(f_ex, 1)

        def final_dve(dve):
            for i in range(12):
                k = NSTREAM + i
                j = (i - 4) // 2
                dst = i * CH if i < 4 else (j * CH if i % 2 == 0 else 4096 + j * CH)
                dve.wait_ge(f_in[i % 2], 16 * (i // 2 + 1))
                if i >= 4:
                    if i % 2 == 0:
                        dve_units(dve, 2 * j, 2 * j + 2)
                    dve.wait_ge(f_ab, 2 * j + 2)
                hi, lo = cols(W0, dst, dst + CH)
                src = stage2[i % 2]
                dve.tensor_copy(hi, src).then_inc(w_hi, 2)
                dve.wait_ge(w_hi, 2 * k + 2)
                dve.tensor_tensor(lo, src, f(hi), ALU.subtract).then_inc(w_lo, 1)
            dve_units(dve, 8, 16)
            dve.wait_ge(w_lo, NCHUNK)
            zeros = prob[:, :, :].rearrange("p m n -> p (m n)")[:, 0:B * KC]
            dve.memset(MB, float("-inf")).then_inc(f_mb0, 1)
            dve.memset(zeros, 0.0).then_inc(f_mb0, 1)
            dve.wait_ge(f_ms, 32)
            dve.wait_ge(f_mb0, 2)
            dve.copy_predicated(MB, staged[:, 0:B * KC].bitcast(I32), zeros).then_inc(f_mb0, 1)
            dve.wait_ge(f_mb0, 3)
            for hb in range(2):
                base = 16 + HALF_UNITS * hb
                for i in range(16):
                    unit_evac_dve(dve, (base + i, i % 4), KOH, g_dst(i // 2, i % 2))
                with dve.Fori(0, 4) as b4:
                    t = dve.snap(b4 + hb * 4)
                    u0 = dve.snap(t * 4 + 16 + 16 * (hb + 1))
                    n4 = dve.snap(t * 4)
                    dve.wait_ge(f_xn, t * 2 + GIVEN)
                    dve.tensor_copy(norm[:, :, :], xs(t)).then_inc(f_xc, 1)
                    context_to_fixed(dve, t, f_xr, t + GIVEN)
                    dve.wait_ge(f_th, t + 1)
                    dve.tensor_tensor(hTl[:, :, :], pj[:, :].rearrange("p (c n) -> p c n", c=2), f(hTh[:, :, :]),
                                      ALU.subtract).then_inc(f_tl, 1)
                    for i in range(4):
                        unit_evac_dve(dve, (u0 + i, i), 512, vo_dst(i), KC)
                    for k in range(5):
                        if k < 4:
                            m = k % 2
                            dve.wait_ge(f_sc, n4 + k + 1)
                            if k >= 2:
                                dve.wait_ge(f_tp, n4 + k - 1)
                            v = prob[:, m, 0:PAIRC].rearrange("p (h k) -> p h k", h=4)
                            bias = MB[:, bass.ds(t * KC, KC)].unsqueeze(1).to_broadcast([P, 4, KC])
                            dve.tensor_tensor(v, sc[m][:, 0:KOH].rearrange("p (h k) -> p h k", h=4)[:, :, 0:KC],
                                              bias, ALU.add).then_inc(f_mb, 1)
                            dve.wait_ge(f_mb, n4 + k + 1)
                            dve.tensor_reduce(nmax[:, m, :], v, AX.X, ALU.max, negate=True).then_inc(f_mx, 1)
                            dve.wait_ge(f_mx, n4 + k + 1)
                            dve.tensor_scalar(nbias[:, m, :], nmax[:, m, :], SCALE_F, None, ALU.mult)\
                                .then_inc(f_nb, 1)
                        if k >= 1:
                            m = (k - 1) % 2
                            dve.wait_ge(f_ph, n4 + k)
                            dve.tensor_tensor(ptl[0:KC, m, :], pt[m][0:KC, :], f(pth[0:KC, m, :]), ALU.subtract)\
                                .then_inc(f_pl, 1)
                        if k < 4:
                            m = k % 2
                            dve.wait_ge(f_ex, n4 + k + 1)
                            dve.reciprocal(rsum[:, m, :], psums[:, m, :]).then_inc(f_rc, 1)
                    dve.wait_ge(f_op, n4 + 4)
                    dve.tensor_tensor(norm[:, :, :], po[:, :].rearrange("p (q c) -> p q c", q=2), norm[:, :, :],
                                      ALU.add)\
                        .then_inc(f_xr, 1)
                    dve.wait_ge(f_xr, t + 1 + GIVEN)
                    for q in range(2):
                        last = dve.bn_stats(stats[:, q, :], norm[:, q, :])
                    last.then_inc(f_st, 1)
                    dve.wait_ge(f_st, t + 1)
                    dve.memset(pace[:, :], 0.0)
                    for q in range(2):
                        last = dve.bn_aggr(mv[:, q, :], stats[:, q, :])
                    last.then_inc(ln_mv, 1)
                    dve.wait_ge(ln_rs, t + 27 * L + 1)
                    dve.wait_ge(out_done, t * 16 + 16)
                    for q in range(2):
                        last = dve.tensor_scalar(yout[:, q, :], norm[:, q, :], mv[:, q, 0:1], rstd[:, q:q + 1],
                                                 ALU.subtract, ALU.mult)
                    last.then_inc(f_xn, 1)
                    dve.wait_ge(f_xn, t * 2 + 1 + GIVEN)
                    dve.tensor_tensor(yout[:, :, :], yout[:, :, :], GB[:, 0:1, :].to_broadcast([P, 2, C]), ALU.mult)\
                        .then_inc(f_xn, 1)
                    dve.wait_ge(f_xn, t * 2 + 2 + GIVEN)
                    dve.tensor_tensor(yout[:, :, :], yout[:, :, :], GB[:, 1:2, :].to_broadcast([P, 2, C]), ALU.add)\
                        .then_inc(f_y, 1)

        def dve_units(dve, first, end):
            for u in range(first, end):
                base = 4096 * (u // 8) + (u % 8) * 512
                unit_evac_dve(dve, (u, u % 4), 512, cols(W1, base, base + 512))

        def final_pool(pool):
            with pool.Fori(0, B) as t:
                for k in range(4):
                    m = k % 2
                    v = prob[:, m, 0:PAIRC].rearrange("p (h k) -> p h k", h=4)
                    pool.wait_ge(f_rc, t * 4 + k + 1)
                    pool.tensor_tensor(v, v, rsum[:, m, :].unsqueeze(2).to_broadcast([P, 4, KC]), ALU.mult)\
                        .then_inc(f_nm, 1)
                ln_rstd(pool, t + 27 * L)
        block = ctx.enter_context(nc.Block())

        @block.sync
        def _(sp):
            sp.sem_inc(out_done, 16)
            sp.dma_start(xres[:, 0:B, :, :], x.rearrange("b (q p) c -> p b q c", p=P)).then_inc(x_in, 16)
            for e, raw in enumerate((ctx_raw0, ctx_raw1)):
                sp.dma_start(raw, ctx_t[e, :, :]).then_inc(ctx_in, 16)
            sp.dma_start(staged[:, :], wts[0, :, :]).then_inc(stg_in, 16)
            with sp.Fori(1, NSTREAM) as k:
                sp.wait_ge(w_lo, k)
                sp.dma_start(staged[:, :], wts[bass.ds(k, 1), :, :].rearrange("o p n -> p (o n)"))\
                    .then_inc(stg_in, 16)
            final_sync(sp)

        def layers(eng, body):
            with eng.Fori(0, L) as l:
                body(l)

        @block.tensor
        def _(pe):
            pe.wait_ge(setup_g, 4)
            pe.wait_ge(w_lo, NA_HIGH)

            def body(l):
                def a_pre(a):
                    ln_turn(pe, a.uses - 2, a.lns)
                    pe_proj(pe, a, ("qk", 0), a.uses - 1, a.lns + 1)
                    pe_proj(pe, a, ("v", 0), a.uses, a.lns + 1)

                def a_slot(a, h, mode, b):
                    if mode == "first":
                        need = {6: 1, 7: 2, 10: 3, 14: 4}
                        if h in need:
                            pe.wait_ge(w_lo, l * PER_LAYER + NA_HIGH + need[h])
                    a_slot_pe(pe, a, h, mode)
                run(pe, 0, l, 3 * l + 1, a_pre, a_slot, H, 5)

                def b_pre(a):
                    ln_turn(pe, a.vuses, a.lns, vb, v_full, v_free)
                    b_qk_pe(pe, 0, a.uses, a.lns + 1, 0)
                run(pe, 1, l, 3 * l + 2, b_pre, lambda a, p, mode, b: b_slot_pe(pe, a, p, mode, b), NPAIR, 5)

                run(pe, 2, l, 3 * l + 3, lambda a: ln_turn(pe, a.uses, a.lns),
                    lambda a, m, mode, b: c_slot_pe(pe, a, m, mode), 8, 2)
            layers(pe, body)
            final_pe(pe)

        @block.scalar
        def _(act):
            def params(l):
                act.dma_start(pk[:, :], par[bass.ds(l, 1), :, :].rearrange("o p n -> p (o n)"))\
                    .then_inc(par_in, 16)
                act.dma_start(brow[:, :, :], rows[bass.ds(l, 1), :, :].rearrange("o r c -> (o r c)")
                              .partition_broadcast(P).rearrange("p (r c) -> p r c", r=3))\
                    .then_inc(par_in, 16)

            act.wait_ge(setup_g, 4)

            def body(l):
                params(l)

                def pre_a(a):
                    ln_hi(act, a.uses - 2)
                    act_proj(act, a, ("qk", 0), a.uses - 1, None)
                    act_proj(act, a, ("v", 0), a.uses, None)
                run(act, 0, l, 3 * l + 1, pre_a, lambda a, h, mode, b: a_slot_act(act, a, h, mode), H, 3)

                def pre_b(a):
                    b_ln_hi(act, a.vuses)
                    act.wait_ge(zeroed, l + 1)
                    b_qk_act(act, 0, a.uses)
                run(act, 1, l, 3 * l + 2, pre_b, lambda a, p, mode, b: b_slot_act(act, a, p, mode), NPAIR, 3)

                run(act, 2, l, 3 * l + 3, lambda a: ln_hi(act, a.uses),
                    lambda a, m, mode, b: c_slot_act(act, a, m, mode), 8, 0)
            layers(act, body)
            final_act(act)

        @block.vector
        def _(dve):
            dve.sem_inc(pj_free, GIVEN)
            dve.sem_inc(v_free, GIVEN)
            dve.sem_inc(f_xr, GIVEN)
            dve.sem_inc(f_xn, GIVEN)
            dve.memset(half[:, :], -0.5).then_inc(setup_v, 1)
            dve.memset(xres[:, B, :, :], 0.0).then_inc(setup_v, 1)
            dve.memset(ones[:, :], 1.0).then_inc(setup_v, 1)
            dve.memset(eps[:, :], EPS).then_inc(setup_v, 1)
            dve.wait_ge(x_in, 16)
            dve.wait_ge(setup_v, 4)

            def body(l):
                def pre_a(a):
                    ln_stats(dve, 0, a.lns)
                    ln_apply(dve, 0, a.lns)
                    dve.wait_ge(par_in, (l + 1) * 32)
                    ln_raw(dve, 0, a.uses - 2)
                    dve_proj(dve, a, ("qk", 0), a.uses - 1)
                    dve_proj(dve, a, ("v", 0), a.uses)
                run(dve, 0, l, 3 * l + 1, pre_a,
                    lambda a, h, mode, b: a_slot_dve(dve, a, h, mode, b), H, 6)

                def pre_b(a):
                    dve.memset(f(vhl[:, :, 1, :, :]), 0.0).then_inc(zeroed, 1)
                    ln_stats(dve, 0, a.lns)
                    context_to_fixed(dve, 0, setup_g, 4)
                    ln_apply(dve, 0, a.lns)
                    ln_raw(dve, 1, a.vuses, vb, v_full, v_free)
                    b_ln_lo(dve, a.vuses)
                    b_qk_dve(dve, 0, a.uses)
                run(dve, 1, l, 3 * l + 2, pre_b,
                    lambda a, p, mode, b: b_slot_dve(dve, a, p, mode, b), NPAIR, 6)

                def pre_c(a):
                    ln_stats(dve, 0, a.lns)
                    ln_apply(dve, 0, a.lns)
                    ln_raw(dve, 2, a.uses)
                run(dve, 2, l, 3 * l + 3, pre_c,
                    lambda a, m, mode, b: c_slot_dve(dve, a, m, mode, b), 8, 3)
            layers(dve, body)
            final_dve(dve)

        @block.gpsimd
        def _(pool):
            pool.sem_inc(ln_hT, GIVEN)
            pool.memset(ident[:, :], 0.0).then_inc(setup_g, 1)
            pool.wait_ge(setup_g, 1)
            pool.affine_select(out=ident[:, :], in_=ident[:, :], compare_op=ALU.not_equal, fill=1.0, base=0,
                               pattern=[[-1, P]], channel_multiplier=1).then_inc(setup_g, 1)
            pool.wait_ge(ctx_in, 32)
            for e, raw in enumerate((ctx_raw0, ctx_raw1)):
                last = pool.tensor_scalar(cTh[:, e, :], raw, 1.0, 1.0, ALU.mult, ALU.mult)
            last.then_inc(setup_g, 1)
            pool.wait_ge(setup_g, 3)
            for e, raw in enumerate((ctx_raw0, ctx_raw1)):
                last = pool.tensor_tensor(cTl[:, e, :], raw, f(cTh[:, e, :]), ALU.subtract)
            last.then_inc(setup_g, 1)
            pool.wait_ge(setup_v, 4)
            for i in range(NA_HIGH):
                split_chunk(pool, W0, (4 + i) * CH, i + 1)

            def body(l):
                def pre(a):
                    ln_rstd(pool, a.lns)
                    ln_lo(pool, a.uses - 2)
                run(pool, 0, l, 3 * l + 1, pre,
                    lambda a, h, mode, b: a_slot_pool(pool, a, h, mode, b, l), H, 3)
                run(pool, 1, l, 3 * l + 2, lambda a: ln_rstd(pool, a.lns),
                    lambda a, p, mode, b: b_slot_pool(pool, a, p, mode, b, l), NPAIR, 4)

                def pre_c(a):
                    ln_rstd(pool, a.lns)
                    ln_lo(pool, a.uses)
                run(pool, 2, l, 3 * l + 3, pre_c,
                    lambda a, m, mode, b: c_slot_pool(pool, a, m, mode, b), 8, 0)
            layers(pool, body)
            final_pool(pool)


def _chunks(v):
    import numpy as np

    def tiles(w, n):
        r = -(-w.shape[0] // 128)
        if w.shape[0] < r * 128:
            w = np.concatenate([w, np.zeros((r * 128 - w.shape[0], w.shape[1]), w.dtype)])
        return w.reshape(r, 128, -1, n).transpose(1, 0, 2, 3)

    def a_chunks(l):
        w = v["L0_xattn_w_qkv"][l]
        q, k, vv = w[:, 0:1024], w[:, 1024:2048], w[:, 2048:3072]
        qk = np.stack([tiles(q, 128), tiles(k, 128)], axis=0).transpose(1, 3, 0, 2, 4)
        vg = tiles(vv, 256).transpose(0, 2, 1, 3)
        o = tiles(v["L0_xattn_w_sa_o"][l], 256)
        o = o.reshape(128, 2, 1024)
        qk = qk.reshape(128, 4, 1024)
        vg = vg.reshape(128, 2, 1024)
        low = [o[:, 0], vg[:, 1], qk[:, 3], o[:, 1]]
        high = [qk[:, 0], qk[:, 1], qk[:, 2], vg[:, 0]]
        return low, high

    def b_chunks(l):
        w = v["L0_xattn_w_kv"][l]
        q = tiles(v["L0_xattn_w_q"][l], 128).transpose(0, 2, 1, 3).reshape(128, 2, 1024)
        k = tiles(w[:, 0:1024], 128).transpose(0, 2, 1, 3).reshape(128, 2, 1024)
        vv = tiles(w[:, 1024:2048], 256).transpose(0, 2, 1, 3).reshape(128, 2, 1024)
        o = tiles(v["L0_xattn_w_ca_o"][l], 256).reshape(128, 2, 1024)
        return [t[:, i] for t in (q, k, vv, o) for i in range(2)]

    def c_chunks(l):
        w1 = tiles(v["L0_xattn_w_ff1"][l], 128).transpose(0, 2, 1, 3).reshape(128, 2, 1024)
        w2 = tiles(v["L0_xattn_w_ff2"][l], 256).reshape(128, 2, 1024)
        return [t[:, i] for t in (w1, w2) for i in range(2)]

    def by_head(w):
        w = np.concatenate([w, np.zeros((256 - w.shape[0], w.shape[1]), w.dtype)])
        return w.reshape(256, 8, 2, 128).transpose(3, 1, 2, 0).reshape(128, 4, 1024)

    wq, wk, wv = (by_head(v[f"L1_xattn_W{n}"]) for n in "qkv")
    wo = v["L1_xattn_Wo"].reshape(8, 2, 128, 256).transpose(2, 0, 1, 3).reshape(128, 4, 1024)
    n_layers = v["L0_xattn_w_qkv"].shape[0]
    out = list(a_chunks(0)[1])
    for l in range(n_layers):
        out += a_chunks(l)[0] + b_chunks(l) + c_chunks(l)
        out += a_chunks(l + 1)[1] if l + 1 < n_layers else [wq[:, i] for i in range(4)]
    out += [wk[:, i] for i in range(4)]
    for i in range(4):
        out += [wv[:, i], wo[:, i]]
    return np.ascontiguousarray(np.stack(out))


def kernel(**inputs):
    import numpy as np
    import concourse.bacc as bacc
    from concourse.bass_utils import run_bass_kernel_spmd

    v = {k: np.asarray(a) for k, a in inputs.items()}
    n = lambda name: v["L0_xattn_" + name]
    ctx_t = np.zeros((2, 128, B + 1, KP), v["ctx_768"].dtype)
    c = v["ctx_768"].transpose(2, 0, 1)
    ctx_t[0, :, :B, :KC] = c[0:128]
    ctx_t[1, 0:64, :B, :KC] = c[128:192]
    column = lambda a: a.reshape(L, -1, 128).transpose(0, 2, 1)
    par = np.concatenate([column(n(m)) for i in (1, 2, 3) for m in (f"ln{i}_g", f"ln{i}_b")]
                         + [column(n("b_ff1"))], axis=2)
    rows = np.stack([n("b_sa_o"), n("b_ca_o"), n("b_ff2")], axis=1)
    arrays = {
        "x": v["x"], "ctx_t": ctx_t.reshape(2, 128, CW), "mask": v["mask_BxS2_if1"], "wts": _chunks(v),
        "par": par, "rows": rows, "rows_f": np.stack([v["L1_xattn_gamma"], v["L1_xattn_beta"]]),
    }
    arrays = {k: np.ascontiguousarray(a) for k, a in arrays.items()}
    nc = bacc.Bacc("TRN2", target_bir_lowering=False, num_devices=1)
    args = [nc.dram_tensor(f"in_{k}", a.shape, mybir.dt.from_np(a.dtype), kind="ExternalInput").ap()
            for k, a in arrays.items()]
    out = nc.dram_tensor("out_y", (B, S, C), F32, kind="ExternalOutput").ap()
    build(nc, *args, out)
    r = run_bass_kernel_spmd(nc, [{f"in_{k}": a for k, a in arrays.items()}], core_ids=[0])
    return r.results[0]["out_y"]
```

```python
from contextlib import ExitStack

import concourse.bass as bass
from concourse import mybir

F32 = mybir.dt.float32
F32R = mybir.dt.float32r
I32 = mybir.dt.int32
ALU = mybir.AluOpType
ACT = mybir.ActivationFunctionType
AX = mybir.AxisListType

P = 128
L = 4
B = 8
S = 256
C = 256
H = 16
D = 64
KC = 77
KP = 78
HF = 8
EPS = 1e-5
SCALE = D ** -0.5
SCALE_F = 256 ** -0.5
NPAIR = H // 2
CH = 1024
NA_LOW, NB, NC, NA_HIGH = 4, 8, 4, 4
PER_LAYER = NA_LOW + NB + NC + NA_HIGH
NSTREAM = NA_HIGH + L * PER_LAYER
NCHUNK = NSTREAM + 12
CW = B * KP
QK_USES = NPAIR * B
LAYER_USES = 2 * QK_USES + B
A_V = {1: (0, 1), 3: (1, 0), 5: (1, 1), 7: (2, 0), 9: (2, 1), 11: (3, None), 15: (0, 0)}
A_LN = 8
A_VNTH = {h: n + 1 for n, h in enumerate(sorted([*A_V, A_LN]))}
A_V_DONE = [A_VNTH[1], A_VNTH[5], A_VNTH[9], A_VNTH[11]]
A_VUSES = 8
B_VUSES = 5
B_V_OF = [1, 2, 3, 5]
LAYER_VUSES = (A_VUSES + B_VUSES) * B
O_AT = 0
QK_AT = [4 * CH, 6 * CH, 7 * CH, 2 * CH]
V_AT = [5 * CH, 5 * CH + 512, 3 * CH, 3 * CH + 512]
LOW_ORDER = [0, 3, 2, 1]


def build(nc, x, ctx_t, mask, wts, par, rows, rows_f, out):
    with ExitStack() as ctx:
        def sb(name, shape, dt=F32):
            return ctx.enter_context(nc.sbuf_tensor(name, shape, dt))

        def sem(name):
            return ctx.enter_context(nc.semaphore(name))

        w0h, w0l = sb("w0h", [P, 8 * CH], F32R), sb("w0l", [P, 8 * CH], F32R)
        w1h, w1l = sb("w1h", [P, 8 * CH], F32R), sb("w1l", [P, 8 * CH], F32R)
        staged = sb("staged", [P, CH])
        xres = sb("xres", [P, B + 1, 2, C])
        norm = sb("norm", [P, 2, C])
        htr = norm
        hTh, hTl = sb("hTh", [P, 2, S], F32R), sb("hTl", [P, 2, S], F32R)
        prob = sb("prob", [P, 2, 512])
        with nc.sbuf_tensor("landed", [P, 6 * CH], F32) as landed:
            pass
        qkh, qkl = sb("qkh", [P, 2, 512], F32R), sb("qkl", [P, 2, 512], F32R)
        vhl = sb("vhl", [P, 2, 2, 4, 128], F32R)
        pth, ptl = sb("pth", [P, 2, 512], F32R), sb("ptl", [P, 2, 512], F32R)
        part = sb("part", [P, S])
        otr = sb("otr", [P, 2, S])
        oth, otl = sb("oth", [P, 2, S], F32R), sb("otl", [P, 2, S], F32R)
        cTh, cTl = sb("cTh", [P, 2, CW], F32R), sb("cTl", [P, 2, CW], F32R)
        brow = sb("brow", [P, 3, C])
        pk = sb("pk", [P, 16])
        pn = sb("pn", [P, 4])
        ident = sb("ident", [P, P])
        stats = sb("stats", [P, 2, 6])
        mv = sb("mv", [P, 2, 2])
        vare = sb("vare", [P, 2])
        rstd = sb("rstd", [P, 2])
        half = sb("half", [P, 2])
        ones = sb("ones", [P, 1])
        eps = sb("eps", [P, 1])
        pace = sb("pace", [P, 1])
        nmax = sb("nmax", [P, 2, 4])
        nbias = sb("nbias", [P, 2, 4])
        psums = sb("psums", [P, 2, 4])
        rsum = sb("rsum", [P, 2, 4])

        sc = [ctx.enter_context(nc.psum_tensor(f"sc{i}", [P, 512], F32)) for i in range(2)]
        pt = [ctx.enter_context(nc.psum_tensor(f"pt{i}", [P, 512], F32)) for i in range(2)]
        pv = [ctx.enter_context(nc.psum_tensor(f"pv{i}", [P, 512], F32)) for i in range(2)]
        pj = ctx.enter_context(nc.psum_tensor("pj", [P, 512], F32))
        po = ctx.enter_context(nc.psum_tensor("po", [P, 512], F32))

        def f(ap):
            return ap.bitcast(F32)

        x_in = sem("x_in")
        par_in = sem("par_in")
        pn_in = sem("pn_in")
        x_rest = sem("x_rest")
        first_in = [sem(f"first_in{i}") for i in range(3)]
        stg_in = sem("stg_in")
        w_hi = sem("w_hi")
        w_lo = sem("w_lo")
        setup_g = sem("setup_g")
        setup_v = sem("setup_v")
        met = sem("met")
        ln_st = sem("ln_st")
        ln_mv = sem("ln_mv")
        ln_ve = sem("ln_ve")
        ln_rs = sem("ln_rs")
        ln_nm = sem("ln_nm")
        ln_hh = sem("ln_hh")
        ln_hT = sem("ln_hT")
        xb = sem("xb")
        pj_full = sem("pj_full")
        pj_hi = sem("pj_hi")
        pj_free = sem("pj_free")
        v_full = sem("v_full")
        v_hi = sem("v_hi")
        v_free = sem("v_free")
        zeroed = sem("zeroed")
        ctx_in = sem("ctx_in")
        ctx_b = sem("ctx_b")
        a_sc = sem("a_sc")
        a_mx = sem("a_mx")
        a_nb = sem("a_nb")
        a_ex = sem("a_ex")
        a_rc = sem("a_rc")
        a_nm = sem("a_nm")
        a_tp = sem("a_tp")
        a_ph = sem("a_ph")
        a_pl = sem("a_pl")
        a_pv = sem("a_pv")
        a_pc = sem("a_pc")
        a_ot = sem("a_ot")
        a_oh = sem("a_oh")
        a_ol = sem("a_ol")
        a_op = sem("a_op")
        a_xr = sem("a_xr")
        b_sc = sem("b_sc")
        b_mx = sem("b_mx")
        b_nb = sem("b_nb")
        b_ex = sem("b_ex")
        b_rc = sem("b_rc")
        b_nm = sem("b_nm")
        b_tp = sem("b_tp")
        b_ph = sem("b_ph")
        b_pl = sem("b_pl")
        b_pv = sem("b_pv")
        b_pc = sem("b_pc")
        b_ot = sem("b_ot")
        b_oh = sem("b_oh")
        b_ol = sem("b_ol")
        b_op = sem("b_op")
        b_xr = sem("b_xr")
        c_f1 = sem("c_f1")
        c_gl = sem("c_gl")
        c_gh = sem("c_gh")
        c_gw = sem("c_gw")
        c_f2 = sem("c_f2")
        c_xr = sem("c_xr")
        f_ms = sem("f_ms")
        f_mb0 = sem("f_mb0")
        f_ab = sem("f_ab")
        f_ah = sem("f_ah")
        f_al = sem("f_al")
        f_sc = sem("f_sc")
        f_mb = sem("f_mb")
        f_mx = sem("f_mx")
        f_nb = sem("f_nb")
        f_ex = sem("f_ex")
        f_rc = sem("f_rc")
        f_nm = sem("f_nm")
        f_tp = sem("f_tp")
        f_ph = sem("f_ph")
        f_pl = sem("f_pl")
        f_op = sem("f_op")
        f_xr = sem("f_xr")
        f_xc = sem("f_xc")
        f_tt = sem("f_tt")
        f_th = sem("f_th")
        f_tl = sem("f_tl")
        f_st = sem("f_st")
        f_xn = sem("f_xn")
        f_y = sem("f_y")
        out_done = sem("out_done")
        f_in = [sem(f"f_in{i}") for i in range(8)]
        fv_ab = sem("fv_ab")
        fv_ah = sem("fv_ah")
        fv_al = sem("fv_al")

        GIVEN = 1

        def barrier(eng, k):
            eng.drain().then_inc(met, 1)
            eng.wait_ge(met, 4 * k)

        def mm3(pe, o, w, m, start, stop, lint=False):
            (wh, wl), (mh, ml) = w, m
            pe.matmul(o, wh, mh, start=start, stop=False, skip_group_check=lint)
            pe.matmul(o, wh, ml, start=False, stop=False, skip_group_check=lint)
            return pe.matmul(o, wl, mh, start=False, stop=stop, skip_group_check=lint)

        def mm2_rest(pe, o, w, m, stop, rest):
            (wh, wl), (mh, ml) = w, m
            pe.matmul(o, wh, mh, start=False, stop=False)
            if rest == "moving":
                return pe.matmul(o, wl[0:64], mh[0:64], start=False, stop=stop)
            return pe.matmul(o, wh[0:64], ml[0:64], start=False, stop=stop)

        def cols(pair, a, b):
            return pair[0][:, a:b], pair[1][:, a:b]

        W0, W1 = (w0h, w0l), (w1h, w1l)

        def following(b, mode):
            return 0 if mode == "last" else b + 1

        class At:

            def __init__(self, eng, l, b, ln_stage):
                keep = (lambda v: v if isinstance(v, int) else eng.snap(v))
                self.b, self.l = b, l
                self.t = keep(l * B + b)
                self.heads = keep(self.t * H)
                self.pairs = keep(self.t * NPAIR)
                base, each = ((1, NPAIR), (QK_USES + 1, NPAIR), (2 * QK_USES, 1))[ln_stage]
                self.uses = keep(l * LAYER_USES + b * each + base)
                self.lns = keep(l * 24 + b + ln_stage * 8)
                self.biases = keep(l * 24 + 8 * ln_stage + b)
                if ln_stage == 0:
                    self.vuses = keep(l * LAYER_VUSES + b * A_VUSES + 2)
                if ln_stage == 1:
                    self.pairs2 = keep(self.t * H)
                    self.vuses = keep(l * LAYER_VUSES + A_VUSES * B + b * B_VUSES + 1)
                    self.contexts = keep(l * B + b)
                if ln_stage == 2:
                    self.vuses = keep(l * LAYER_VUSES + LAYER_VUSES + 2)

        def xs(b):
            if isinstance(b, int):
                return xres[:, b, :, :]
            return xres[:, bass.ds(b, 1), :, :].rearrange("p o q c -> p (o q) c")

        def ln_stats(dve, b, n):
            for q in range(2):
                last = dve.bn_stats(stats[:, q, :], xs(b)[:, q, :])
            last.then_inc(ln_st, 1)
            dve.wait_ge(ln_st, n + 1)
            dve.memset(pace[:, :], 0.0)
            for q in range(2):
                last = dve.bn_aggr(mv[:, q, :], stats[:, q, :])
            last.then_inc(ln_mv, 1)

        def ln_rstd(pool, n):
            pool.wait_ge(ln_mv, n + 1)
            pool.tensor_tensor(vare[:, :], mv[:, :, 1], eps[:, :].to_broadcast([P, 2]), ALU.add).then_inc(ln_ve, 1)
            pool.wait_ge(ln_ve, n + 1)
            pool.tensor_tensor(rstd[:, :], vare[:, :], half[:, :], ALU.pow).then_inc(ln_rs, 1)

        def ln_apply(dve, b, n):
            dve.wait_ge(ln_rs, n + 1)
            dve.wait_ge(ln_hT, n + GIVEN)
            for q in range(2):
                last = dve.tensor_scalar(norm[:, q, :], xs(b)[:, q, :], mv[:, q, 0:1], rstd[:, q:q + 1],
                                         ALU.subtract, ALU.mult)
            last.then_inc(ln_nm, 1)

        def ln_turn(pe, use, n, bank=pj, full=pj_full, free=pj_free):
            pe.wait_ge(ln_nm, n + 1)
            pe.wait_ge(free, use - 1 + GIVEN)
            for c in range(2):
                for q in range(2):
                    last = pe.transpose(bank[:, c * S + q * P:c * S + (q + 1) * P],
                                        norm[:, q, c * P:(c + 1) * P], ident[:, :])
            last.then_inc(full, 1)

        def ln_raw(dve, st, use, bank=pj, full=pj_full, hi=pj_hi, free=pj_free):
            dve.wait_ge(full, use)
            gb = pk[:, (st - 1) * 4:st * 4] if st else pn[:, :]
            for c in range(2):
                dve.tensor_scalar(htr[:, c, :], bank[:, c * S:(c + 1) * S], gb[:, c:c + 1],
                                  gb[:, 2 + c:3 + c], ALU.mult, ALU.add).then_inc((hi, free)[c], 1)

        def ln_hi(act, use, free=pj_free):
            act.wait_ge(free, use + GIVEN)
            act.activation(hTh[:, :, :], htr[:, :, :], ACT.Copy).then_inc(ln_hh, 1)

        def ln_lo(dve, n):
            dve.wait_ge(ln_hh, n + 1)
            dve.tensor_tensor(hTl[:, :, :], htr[:, :, :], f(hTh[:, :, :]), ALU.subtract).then_inc(ln_hT, 1)

        def first_dst(k):
            return cols(W0, (4 + k) * CH, (5 + k) * CH)

        def split_half(pool, reg, dst, before, i):
            n, half_ = before + i // 2, i % 2
            if half_ == 0:
                pool.wait_ge(stg_in, (n - 2) * 16)
            src = staged[:, half_ * 512:(half_ + 1) * 512]
            if isinstance(dst, int):
                hi, lo = (w[:, dst + half_ * 512:dst + half_ * 512 + 512] for w in reg)
            else:
                hi, lo = (w[:, bass.ds(dst + half_ * 512, 512)] for w in reg)
            pool.tensor_tensor(hi, src, ones[:, :].to_broadcast([P, 512]), ALU.mult).then_inc(w_hi, 1)
            pool.wait_ge(w_hi, n * 2 + half_ + 1)
            last = pool.tensor_tensor(lo, src, f(hi), ALU.subtract)
            if half_:
                last.then_inc(w_lo, 1)

        LOW_SLOT = {0: 0, 1: 1, 3: 2, 4: 3, 6: 4, 7: 5, 9: 6, 10: 7}

        def low_half(i):
            at = LOW_ORDER[i // 2] * CH + i % 2 * 512
            return staged[:, i % 2 * 512:i % 2 * 512 + 512], cols(W0, at, at + 512)

        def low_hi(act, l, i):
            src, (hi, lo) = low_half(i)
            if i % 2 == 0:
                act.wait_ge(stg_in, (l * PER_LAYER + NA_HIGH + i // 2 - 2) * 16)
            act.activation(hi, src, ACT.Copy).then_inc(w_hi, 1)

        def low_lo(pool, l, i):
            src, (hi, lo) = low_half(i)
            pool.wait_ge(w_hi, (l * PER_LAYER + NA_HIGH) * 2 + i + 1)
            last = pool.tensor_tensor(lo, src, f(hi), ALU.subtract)
            if i % 2:
                last.then_inc(w_lo, 1)

        def a_qk_pe(pe, i, use, ln):
            pe.wait_ge(pj_free, use - 1 + GIVEN)
            pe.wait_ge(ln_hT, ln + GIVEN)
            at = QK_AT[i // 2] + (i % 2) * 512
            for qk in range(2):
                for c in range(2):
                    w = at + qk * 256 + c * P
                    last = mm3(pe, pj[:, qk * S:(qk + 1) * S], cols(W0, w, w + P),
                               (hTh[:, c, :], hTl[:, c, :]), c == 0, c == 1)
            last.then_inc(pj_full, 1)

        def a_qk_act(act, i, use):
            act.wait_ge(pj_full, use)
            act.activation(qkh[:, i % 2, :], pj[:, :], ACT.Copy).then_inc(pj_hi, 1)

        def a_qk_dve(dve, i, use):
            dve.wait_ge(pj_hi, use)
            dve.tensor_tensor(qkl[:, i % 2, :], pj[:, :], f(qkh[:, i % 2, :]), ALU.subtract).then_inc(pj_free, 1)

        kbk = vhl[:, :, 1, :, :].rearrange("p m h d -> p m (h d)")
        vb = pv[1]

        def a_v_pe(pe, v, use, ln):
            i, tile = v
            pe.wait_ge(v_free, use - 1 + GIVEN)
            pe.wait_ge(ln_hT, ln + GIVEN)
            for kt in ((0, 1) if tile is None else (tile,)):
                for c in range(2):
                    w = V_AT[i] + c * 256
                    last = mm3(pe, vb[:, kt * 256:(kt + 1) * 256],
                               (hTh[:, c, kt * P:(kt + 1) * P], hTl[:, c, kt * P:(kt + 1) * P]),
                               cols(W0, w, w + 256), c == 0, c == 1)
            last.then_inc(v_full, 1)

        def v_parts(v):
            i, tile = v
            if tile is None:
                return (vhl[:, i % 2, :, :, 0:D], vhl[:, i % 2, :, :, D:2 * D],
                        vb[:, :].rearrange("p (k h d) -> p k h d", k=2, h=4))
            return (vhl[:, i % 2, tile, :, 0:D], vhl[:, i % 2, tile, :, D:2 * D],
                    vb[:, tile * 256:(tile + 1) * 256].rearrange("p (h d) -> p h d", h=4))

        def a_v_act(act, v, use):
            hi, lo, src = v_parts(v)
            act.wait_ge(v_full, use)
            act.activation(hi, src, ACT.Copy).then_inc(v_hi, 1)

        def a_v_dve(dve, v, use):
            hi, lo, src = v_parts(v)
            dve.wait_ge(v_hi, use)
            dve.tensor_tensor(lo, src, f(hi), ALU.subtract).then_inc(v_free, 1)

        def a_slot_pe(pe, a, h, mode):
            new, old = mode != "tail", (lambda k: h - k >= 0 or mode != "first")
            N = lambda k: a.heads + (h - k) + 1
            if old(2) and (new or h - 2 < 0):
                m = h % 2
                pe.wait_ge(a_nm, N(2))
                if old(4):
                    pe.wait_ge(a_pl, N(4))
                for kt in range(2):
                    for q in range(2):
                        last = pe.transpose(pt[m][:, kt * S + q * P:kt * S + (q + 1) * P],
                                            prob[:, m, q * S + kt * P:q * S + (kt + 1) * P], ident[:, :])
                last.then_inc(a_tp, 1)
            if new:
                p, j = h // 2, h % 2
                pe.wait_ge(pj_free, a.uses + p + GIVEN)
                if old(2):
                    pe.wait_ge(a_ex, N(2))
                r = slice(D * j, D * j + D)
                for q in range(2):
                    qs = slice(q * P, (q + 1) * P)
                    last = mm3(pe, sc[h % 2][:, q * S:(q + 1) * S],
                               (qkh[r, p % 2, qs], qkl[r, p % 2, qs]),
                               (qkh[r, p % 2, S:2 * S], qkl[r, p % 2, S:2 * S]), True, True)
                last.then_inc(a_sc, 1)
            if old(3) and (new or h - 3 < 0):
                hh = (h - 3) % H
                m = hh % 2
                pe.wait_ge(a_pl, N(3))
                pe.wait_ge(v_free, a.vuses + A_V_DONE[hh // 4] - (A_VUSES if h < 3 else 0) + GIVEN)
                if old(4):
                    pe.wait_ge(a_ot, N(4))
                for kt in range(2):
                    v = vhl[:, (hh // 4) % 2, kt, hh % 4, :]
                    pe.matmul(pv[0][:, 0:S], v, pth[:, m, kt * S:(kt + 1) * S], start=kt == 0, stop=False)
                    last = pe.matmul(pv[0][:, 0:S], v, ptl[:, m, kt * S:(kt + 1) * S], start=False,
                                     stop=kt == 1)
                last.then_inc(a_pv, 1)
            if new and h == A_LN:
                ln_turn(pe, a.vuses + A_VNTH[h], a.lns + 1, vb, v_full, v_free)
            if new and h % 2 == 0 and not (h == 14 and mode == "last"):
                p = h // 2
                a_qk_pe(pe, (p + 1) % NPAIR, a.uses + p + 1, a.lns + (2 if h == 14 else 1))
            if h % 2 == 1 and old(7) and (new or h - 7 < 0):
                p = ((h - 7) // 2) % NPAIR
                pe.wait_ge(a_ol, a.pairs + (h - 7) // 2 + 1)
                if p == 0 and mode != "first":
                    pe.wait_ge(a_xr, a.t)
                for q in range(2):
                    qs = slice(q * P, (q + 1) * P)
                    w = O_AT + p * 256
                    last = mm3(pe, po[:, q * C:(q + 1) * C], (oth[:, p % 2, qs], otl[:, p % 2, qs]),
                               cols(W0, w, w + 256), p == 0 and q == 0, p == NPAIR - 1, lint=True)
                last.then_inc(a_op, 1)
            if mode == "last" and h == 15:
                pe.wait_ge(w_lo, a.l * PER_LAYER + NA_HIGH + NA_LOW + 3)
                pe.wait_ge(setup_g, 5)
                b_qk_pe(pe, 0, a.uses + NPAIR, a.lns + 2, 0)
            elif new and h in A_V:
                a_v_pe(pe, A_V[h], a.vuses + A_VNTH[h], a.lns + (2 if h == 15 else 1))

        def a_slot_act(act, a, h, mode):
            new, old = mode != "tail", (lambda k: h - k >= 0 or mode != "first")
            N = lambda k: a.heads + (h - k) + 1
            if old(2) and (new or h - 2 < 0):
                m = h % 2
                act.wait_ge(a_tp, N(2))
                if old(4):
                    act.wait_ge(a_pv, N(4))
                act.activation(pth[:, m, :], pt[m][:, :], ACT.Copy).then_inc(a_ph, 1)
            if old(3) and (new or h - 3 < 0):
                j = (h - 3) % 2
                act.wait_ge(a_pv, N(3))
                if old(4):
                    act.wait_ge(a_ot, N(4))
                src, dst = (slice(D, P), slice(0, D)) if j == 0 else (slice(0, D), slice(D, P))
                act.activation(part[dst, :], pv[0][src, 0:S], ACT.Copy).then_inc(a_pc, 1)
            if mode == "tail" and h == 0:
                act.wait_ge(zeroed, a.l * 2 + 1)
                act.wait_ge(a_sc, a.heads)
                b_qk_act(act, 0, a.uses)
            if new:
                m = h % 2
                act.wait_ge(a_nb, N(0))
                if old(2):
                    act.wait_ge(a_tp, N(2))
                for q in range(2):
                    last = act.activation(prob[:, m, q * S:(q + 1) * S], sc[m][:, q * S:(q + 1) * S], ACT.Exp,
                                          bias=nbias[:, m, q:q + 1], scale=SCALE,
                                          accum_out=psums[:, m, q:q + 1])
                last.then_inc(a_ex, 1)
                if h % 2 == 0 and not (h == 14 and mode == "last"):
                    if h >= 1 or mode != "first":
                        act.wait_ge(a_sc, a.heads + h)
                    a_qk_act(act, (h // 2 + 1) % NPAIR, a.uses + h // 2 + 1)
                if h in A_V and not (h == 15 and mode == "last"):
                    if h > 3 or mode != "first":
                        act.wait_ge(a_pv, a.heads + h - 3)
                    a_v_act(act, A_V[h], a.vuses + A_VNTH[h])
                if h == 13:
                    ln_hi(act, a.vuses + A_VNTH[A_LN], v_free)
                if mode == "first" and h in LOW_SLOT:
                    low_hi(act, a.l, LOW_SLOT[h])

        def a_slot_dve(dve, a, h, mode, b):
            new, old = mode != "tail", (lambda k: h - k >= 0 or mode != "first")
            N = lambda k: a.heads + (h - k) + 1
            m = h % 2
            if old(1) and (new or h - 1 < 0):
                n = (h - 1) % 2
                dve.wait_ge(a_ex, N(1))
                dve.reciprocal(rsum[:, n, 0:2], psums[:, n, 0:2]).then_inc(a_rc, 1)
            if new and h == 0:
                a_v_dve(dve, A_V[15], a.vuses)
            if new and h % 2 == 1 and not (h == 15 and mode == "last"):
                a_qk_dve(dve, ((h + 1) // 2) % NPAIR, a.uses + (h + 1) // 2)
            if new and h - 1 in A_V:
                a_v_dve(dve, A_V[h - 1], a.vuses + A_VNTH[h - 1])
            if new and h == 14:
                ln_lo(dve, a.lns + 1)
            if h == 6 and mode != "first":
                residual(dve, a_op, a.pairs, a_xr, b - 1, a.biases)
            if new:
                dve.wait_ge(a_sc, N(0))
                dve.tensor_reduce(nmax[:, m, 0:2], sc[m][:, :].rearrange("p (q k) -> p q k", q=2), AX.X, ALU.max,
                                  negate=True).then_inc(a_mx, 1)
                dve.wait_ge(a_mx, N(0))
                dve.tensor_scalar(nbias[:, m, 0:2], nmax[:, m, 0:2], SCALE, None, ALU.mult)\
                    .then_inc(a_nb, 1)
            if old(2) and (new or h - 2 < 0):
                dve.wait_ge(a_ph, N(2))
                dve.tensor_tensor(ptl[:, m, :], pt[m][:, :], f(pth[:, m, :]), ALU.subtract)\
                    .then_inc(a_pl, 1)
            if old(3) and (new or h - 3 < 0):
                hh = (h - 3) % H
                p, j = hh // 2, hh % 2
                dve.wait_ge(a_pc, N(3))
                if j == 0 and old(7):
                    dve.wait_ge(a_ol, a.pairs + (h - 3) // 2 - 1)
                r = slice(D * j, D * j + D)
                dve.tensor_tensor(otr[r, p % 2, :], pv[0][r, 0:S], part[r, :], ALU.add).then_inc(a_ot, 1)
            if mode == "tail" and h == 0:
                dve.wait_ge(a_pv, a.heads - 4)
                dve.memset(f(kbk[:, 0, 0:4 * KP]), 0.0).then_inc(zeroed, 1)
                b_qk_dve(dve, 0, a.uses)
            if mode == "tail" and h == 1:
                dve.wait_ge(setup_g, 5)
                context_to_fixed(dve, 0, a_sc, a.heads)
            if mode == "tail" and h == 3:
                dve.wait_ge(a_pv, a.heads)
                dve.memset(f(kbk[:, 1, 0:4 * KP]), 0.0).then_inc(zeroed, 1)
            if mode == "first" and h == 5:
                dve.wait_ge(x_rest, 16)
                dve.wait_ge(par_in, a.l * 32 + 32)
            if new and h == 5:
                ln_stats(dve, following(b, mode), a.lns + 1)
            if new and h == 7:
                ln_apply(dve, following(b, mode), a.lns + 1)
            if new and h == A_LN:
                ln_raw(dve, 1 if mode == "last" else 0, a.vuses + A_VNTH[A_LN], vb, v_full, v_hi, v_free)

        def residual(dve, full, count, done, b, xbs):
            dve.wait_ge(full, count)
            dve.wait_ge(xb, xbs)
            dve.tensor_tensor(xs(b), po[:, :].rearrange("p (q c) -> p q c", q=2), xs(b), ALU.add)\
                .then_inc(done, 1)

        def add_bias(pool, b, st):
            bias = brow[:, st:st + 1, :].to_broadcast([P, 2, C])
            pool.tensor_tensor(xs(b), xs(b), bias, ALU.add).then_inc(xb, 1)

        def pair_split(pool, out_sem, count_out, hi_sem, lo_sem, count, m):
            pool.wait_ge(out_sem, count_out)
            pool.tensor_tensor(oth[:, m, :], otr[:, m, :], ones[:, :].to_broadcast([P, S]), ALU.mult)\
                .then_inc(hi_sem, 1)
            pool.wait_ge(hi_sem, count)
            pool.tensor_tensor(otl[:, m, :], otr[:, m, :], f(oth[:, m, :]), ALU.subtract)\
                .then_inc(lo_sem, 1)

        def a_slot_pool(pool, a, h, mode, b, l):
            new, old = mode != "tail", (lambda k: h - k >= 0 or mode != "first")
            N = lambda k: a.heads + (h - k) + 1
            if old(1) and (new or h - 1 < 0):
                v = prob[:, (h - 1) % 2, :].rearrange("p (q k) -> p q k", q=2)
                pool.wait_ge(a_rc, N(1))
                pool.tensor_tensor(v, v, rsum[:, (h - 1) % 2, 0:2].unsqueeze(2).to_broadcast([P, 2, S]),
                                   ALU.mult).then_inc(a_nm, 1)
            if h % 2 == 1 and old(5) and (new or h - 5 < 0):
                g = a.pairs + (h - 5) // 2
                if old(9):
                    pool.wait_ge(a_op, g - 1)
                pair_split(pool, a_ot, N(4), a_oh, a_ol, g + 1, ((h - 5) // 2) % 2)
            if mode == "first" and h - 1 in LOW_SLOT:
                low_lo(pool, l, LOW_SLOT[h - 1])
            if new and h == 6:
                ln_rstd(pool, a.lns + 1)
            if new and h in (12, 14):
                split_half(pool, W1, b * CH, l * PER_LAYER + b + NA_HIGH + NA_LOW, h // 14)
            if new and h == 8:
                if mode == "first":
                    pool.wait_ge(par_in, a.l * 32 + 32)
                pool.wait_ge(ln_nm, a.lns + 1)
                add_bias(pool, b, 0)

        BQ, BK, BV, BO = 0, 2 * CH, 4 * CH, 6 * CH


        def ctxs(t, e, b, n):
            if isinstance(b, int):
                return t[:, e, b * KP:b * KP + n]
            return t[:, e, bass.ds(b * KP, n)]

        cbh = qkh[:, :, S:S + KP]
        cbl = qkl[:, :, S:S + KP]

        def b_qk_pe(pe, i, use, ln, ctx_b):
            pe.wait_ge(pj_free, use - 1 + GIVEN)
            pe.wait_ge(ln_hT, ln + GIVEN)
            for c in range(2):
                w = BQ + i * 256 + c * P
                mm3(pe, pj[:, 0:S], cols(W1, w, w + P), (hTh[:, c, :], hTl[:, c, :]), c == 0, c == 1)
            w = BK + i * 256
            mm3(pe, pj[:, S:S + KP], cols(W1, w, w + P),
                (ctxs(cTh, 0, ctx_b, KP), ctxs(cTl, 0, ctx_b, KP)), True, False)
            last = mm2_rest(pe, pj[:, S:S + KP], cols(W1, w + P, w + 2 * P), (ctxs(cTh, 1, ctx_b, KP), None),
                            True, "moving")
            last.then_inc(pj_full, 1)

        def b_qk_act(act, i, use):
            act.wait_ge(pj_full, use)
            m = i % 2
            act.activation(qkh[:, m, 0:S], pj[:, 0:S], ACT.Copy)
            for j in range(2):
                r = slice(D * j, D * j + D)
                last = act.activation(kbk[r, m, j * KP:(j + 1) * KP], pj[r, S:S + KP], ACT.Copy)
            last.then_inc(pj_hi, 1)

        def b_qk_dve(dve, i, use):
            dve.wait_ge(pj_hi, use)
            m = i % 2
            dve.tensor_tensor(qkl[:, m, 0:S], pj[:, 0:S], f(qkh[:, m, 0:S]), ALU.subtract)
            for j in range(2):
                r = slice(D * j, D * j + D)
                last = dve.tensor_tensor(kbk[r, m, 2 * KP + j * KP:2 * KP + (j + 1) * KP],
                                         pj[r, S:S + KP], f(kbk[r, m, j * KP:(j + 1) * KP]), ALU.subtract)
            last.then_inc(pj_free, 1)

        def b_v_pe(pe, i, use):
            pe.wait_ge(v_free, use - 1 + GIVEN)
            w = BV + i * 512
            mm3(pe, vb[0:KC, 0:256], (cbh[:, 0, 0:KC], cbl[:, 0, 0:KC]), cols(W1, w, w + 256), True, False)
            last = mm2_rest(pe, vb[0:KC, 0:256], (cbh[:, 1, 0:KC], None), cols(W1, w + 256, w + 512), True,
                            "stationary")
            last.then_inc(v_full, 1)

        def b_v_act(act, i, use):
            act.wait_ge(v_full, use)
            act.activation(vhl[0:KC, i % 2, 0, :, 0:D], vb[0:KC, 0:256].rearrange("p (h d) -> p h d", h=4),
                           ACT.Copy).then_inc(v_hi, 1)

        def b_v_dve(dve, i, use):
            dve.wait_ge(v_hi, use)
            dve.tensor_tensor(vhl[0:KC, i % 2, 0, :, D:2 * D],
                              vb[0:KC, 0:256].rearrange("p (h d) -> p h d", h=4),
                              f(vhl[0:KC, i % 2, 0, :, 0:D]), ALU.subtract).then_inc(v_free, 1)

        def b_slot_pe(pe, a, p, mode, b):
            new, old = mode != "tail", (lambda k: p - k >= 0 or mode != "first")
            N = lambda k: a.pairs + (p - k) + 1
            if old(2) and (new or p - 2 < 0):
                m = p % 2
                pe.wait_ge(b_nm, N(2))
                if old(4):
                    pe.wait_ge(b_pl, N(4))
                for j in range(2):
                    for q in range(2):
                        last = pe.transpose(pt[m][0:KC, j * S + q * P:j * S + (q + 1) * P],
                                            prob[:, m, (q * 2 + j) * KC:(q * 2 + j + 1) * KC], ident[:, :])
                last.then_inc(b_tp, 1)
            if new:
                nxt = p == 7
                if not (nxt and mode == "last"):
                    b_qk_pe(pe, (p + 1) % NPAIR, a.uses + p + 1, a.lns + (2 if nxt else 1), b + 1 if nxt else b)
                m = p % 2
                pe.wait_ge(pj_free, a.uses + p + GIVEN)
                if old(2):
                    pe.wait_ge(b_ex, N(2))
                for q in range(2):
                    qs = slice(q * P, (q + 1) * P)
                    last = mm3(pe, sc[m][:, q * 2 * KP:(q + 1) * 2 * KP], (qkh[:, m, qs], qkl[:, m, qs]),
                               (kbk[:, m, 0:2 * KP], kbk[:, m, 2 * KP:4 * KP]), True, True)
                last.then_inc(b_sc, 1)
            if old(3) and (new or p - 3 < 0):
                pp = (p - 3) % NPAIR
                m = pp % 2
                pe.wait_ge(b_pl, N(3))
                pe.wait_ge(v_free, a.vuses + B_V_OF[pp // 2] - (B_VUSES if p < 3 else 0) + GIVEN)
                if old(4):
                    pe.wait_ge(b_ot, a.pairs2 + (p - 4) * 2 + 2)
                for j in range(2):
                    v = vhl[0:KC, (pp // 2) % 2, 0, (pp % 2) * 2 + j, :]
                    o = pv[0][:, j * S:(j + 1) * S]
                    pe.matmul(o, v, pth[0:KC, m, j * S:(j + 1) * S], start=True, stop=False)
                    last = pe.matmul(o, v, ptl[0:KC, m, j * S:(j + 1) * S], start=False, stop=True)
                last.then_inc(b_pv, 1)
            if new and p % 2 == 0:
                if p == 0:
                    pe.wait_ge(ctx_b, a.contexts + 1)
                b_v_pe(pe, p // 2, a.vuses + B_V_OF[p // 2])
            if new and p == 5:
                ln_turn(pe, a.vuses + 4, a.lns + 1, vb, v_full, v_free)
            if old(5) and (new or p - 5 < 0):
                pp = (p - 5) % NPAIR
                pe.wait_ge(b_ol, N(5))
                if pp == 0 and mode != "first":
                    pe.wait_ge(b_xr, a.t)
                for q in range(2):
                    qs = slice(q * P, (q + 1) * P)
                    w = BO + pp * 256
                    last = mm3(pe, po[:, q * C:(q + 1) * C], (oth[:, pp % 2, qs], otl[:, pp % 2, qs]),
                               cols(W1, w, w + 256), pp == 0 and q == 0, pp == NPAIR - 1, lint=True)
                last.then_inc(b_op, 1)

        def b_slot_act(act, a, p, mode):
            new, old = mode != "tail", (lambda k: p - k >= 0 or mode != "first")
            N = lambda k: a.pairs + (p - k) + 1
            if old(2) and (new or p - 2 < 0):
                m = p % 2
                act.wait_ge(b_tp, N(2))
                if old(4):
                    act.wait_ge(b_pv, N(4))
                act.activation(pth[0:KC, m, :], pt[m][0:KC, :], ACT.Copy).then_inc(b_ph, 1)
            if new:
                if not (p == 7 and mode == "last"):
                    if p >= 1 or mode != "first":
                        act.wait_ge(b_sc, a.pairs + p)
                    b_qk_act(act, (p + 1) % NPAIR, a.uses + p + 1)
                if p == 6:
                    ln_hi(act, a.vuses + 4, v_free)
            if old(3) and (new or p - 3 < 0):
                act.wait_ge(b_pv, N(3))
                if old(4):
                    act.wait_ge(b_ot, a.pairs2 + (p - 4) * 2 + 2)
                for j in range(2):
                    src, dst = (slice(D, P), slice(0, D)) if j == 0 else (slice(0, D), slice(D, P))
                    last = act.activation(part[dst, :], pv[0][src, j * S:(j + 1) * S], ACT.Copy)
                last.then_inc(b_pc, 1)
            if new:
                m = p % 2
                act.wait_ge(b_nb, N(0))
                if old(2):
                    act.wait_ge(b_tp, N(2))
                for k in range(4):
                    q, j = k // 2, k % 2
                    last = act.activation(prob[:, m, k * KC:(k + 1) * KC],
                                          sc[m][:, q * 2 * KP + j * KP:q * 2 * KP + j * KP + KC], ACT.Exp,
                                          bias=nbias[:, m, k:k + 1], scale=SCALE,
                                          accum_out=psums[:, m, k:k + 1])
                last.then_inc(b_ex, 1)
            if new and p % 2 == 0:
                if old(3):
                    act.wait_ge(b_pv, N(3))
                b_v_act(act, p // 2, a.vuses + B_V_OF[p // 2])

        def b_slot_dve(dve, a, p, mode, b):
            new, old = mode != "tail", (lambda k: p - k >= 0 or mode != "first")
            N = lambda k: a.pairs + (p - k) + 1
            m = p % 2
            if old(1) and (new or p - 1 < 0):
                n = (p - 1) % 2
                dve.wait_ge(b_ex, N(1))
                dve.reciprocal(rsum[:, n, :], psums[:, n, :]).then_inc(b_rc, 1)
            if new and p % 2 == 1:
                b_v_dve(dve, p // 2, a.vuses + B_V_OF[p // 2])
            if p == 5 and mode != "first":
                residual(dve, b_op, a.pairs, b_xr, b - 1, a.biases)
            if old(2) and (new or p - 2 < 0):
                dve.wait_ge(b_ph, N(2))
                dve.tensor_tensor(ptl[0:KC, m, :], pt[m][0:KC, :], f(pth[0:KC, m, :]), ALU.subtract)\
                    .then_inc(b_pl, 1)
            if new:
                dve.wait_ge(b_sc, N(0))
                dve.tensor_reduce(nmax[:, m, :], sc[m][:, 0:4 * KP].rearrange("p (g k) -> p g k", g=4)[:, :, 0:KC],
                                  AX.X, ALU.max, negate=True).then_inc(b_mx, 1)
                dve.wait_ge(b_mx, N(0))
                dve.tensor_scalar(nbias[:, m, :], nmax[:, m, :], SCALE, None, ALU.mult).then_inc(b_nb, 1)
                if not (p == 7 and mode == "last"):
                    b_qk_dve(dve, (p + 1) % NPAIR, a.uses + p + 1)
                if p == 6:
                    ln_lo(dve, a.lns + 1)
            if p == 7 and mode != "last":
                context_to_fixed(dve, b + 1, v_free, a.vuses + B_VUSES + GIVEN)
            if old(3) and (new or p - 3 < 0):
                n = (p - 3) % 2
                dve.wait_ge(b_pc, N(3))
                if old(5):
                    dve.wait_ge(b_ol, N(5))
                for j in range(2):
                    r = slice(D * j, D * j + D)
                    dve.tensor_tensor(otr[r, n, :], pv[0][r, j * S:(j + 1) * S], part[r, :], ALU.add)\
                        .then_inc(b_ot, 1)
            if new:
                if p == 1:
                    ln_stats(dve, following(b, mode), a.lns + 1)
                if p == 3:
                    ln_apply(dve, following(b, mode), a.lns + 1)
                if p == 5:
                    ln_raw(dve, 2 if mode == "last" else 1, a.vuses + 4, vb, v_full, v_hi, v_free)

        def context_to_fixed(dve, b, free, value):
            dve.wait_ge(free, value)
            for src, dst in ((cTh, cbh), (cTl, cbl)):
                last = dve.tensor_copy(dst, f(src[:, :, b * KP:(b + 1) * KP]) if isinstance(b, int)
                                       else f(src[:, :, bass.ds(b * KP, KP)]))
            last.then_inc(ctx_b, 1)

        def b_slot_pool(pool, a, p, mode, b, l):
            new, old = mode != "tail", (lambda k: p - k >= 0 or mode != "first")
            N = lambda k: a.pairs + (p - k) + 1
            if old(1) and (new or p - 1 < 0):
                n = (p - 1) % 2
                pool.wait_ge(b_rc, N(1))
                v = prob[:, n, 0:4 * KC].rearrange("p (g k) -> p g k", g=4)
                pool.tensor_tensor(v, v, rsum[:, n, :].unsqueeze(2).to_broadcast([P, 4, KC]), ALU.mult)\
                    .then_inc(b_nm, 1)
            if old(4) and (new or p - 4 < 0):
                if old(6):
                    pool.wait_ge(b_op, N(6))
                pair_split(pool, b_ot, a.pairs2 + (p - 4) * 2 + 2, b_oh, b_ol, N(4), p % 2)
            if new and p in (0, 4):
                split_half(pool, W0, b * CH, l * PER_LAYER + b + NA_HIGH + NA_LOW + NB, p // 4)
            if new and p == 2:
                ln_rstd(pool, a.lns + 1)
            if new and p == 5:
                pool.wait_ge(ln_nm, a.lns + 1)
                add_bias(pool, b, 1)

        g_raw = [prob[:, 0, 0:S], prob[:, 0, S:2 * S], prob[:, 1, 0:S], prob[:, 1, S:2 * S]]
        g_hi = [pth[:, i // 2, (i % 2) * S:(i % 2 + 1) * S] for i in range(4)]
        g_lo = [ptl[:, i // 2, (i % 2) * S:(i % 2 + 1) * S] for i in range(4)]
        f1 = [sc[0], sc[1], pt[0], pt[1]]

        def c_slot_pe(pe, a, m, mode):
            new, old = mode != "tail", (lambda k: m - k >= 0 or mode != "first")
            N = lambda k: a.pairs + (m - k) + 1

            def project():
                mm_, i = (m - 3) % 8, (m - 3) % 4
                pe.wait_ge(c_gw, N(3))
                if mm_ == 0 and mode != "first":
                    pe.wait_ge(c_xr, a.t)
                for q in range(2):
                    w = 2 * CH + mm_ * 256
                    last = mm3(pe, po[:, q * C:(q + 1) * C],
                               (g_hi[i][:, q * P:(q + 1) * P], g_lo[i][:, q * P:(q + 1) * P]),
                               cols(W0, w, w + 256), mm_ == 0 and q == 0, mm_ == 7, lint=True)
                last.then_inc(c_f2, 1)
            projects = old(3) and (new or m - 3 < 0)
            if projects and m == 0:
                project()
            if new:
                pe.wait_ge(ln_hT, a.lns + 1 + GIVEN)
                if old(4):
                    pe.wait_ge(c_gl, N(4))
                for c in range(2):
                    w = m * 256 + c * P
                    last = mm3(pe, f1[m % 4][:, 0:S], cols(W0, w, w + P), (hTh[:, c, :], hTl[:, c, :]),
                               c == 0, c == 1)
                last.then_inc(c_f1, 1)
            if projects and m > 0:
                project()
            if new and m == 4:
                ln_turn(pe, a.uses + 1, a.lns + 1)
            if mode == "tail" and m == 0:
                a_qk_pe(pe, 0, a.uses + 1, a.lns + 1)
            if mode == "tail" and m == 1:
                a_v_pe(pe, A_V[15], a.vuses, a.lns + 1)

        def c_slot_act(act, a, m, mode):
            N = lambda k: a.pairs + (m - k) + 1
            if mode == "tail":
                if m == 0:
                    a_qk_act(act, 0, a.uses + 1)
                else:
                    a_v_act(act, A_V[15], a.vuses)
                return
            act.wait_ge(c_f1, N(0))
            if m == 7:
                ln_hi(act, a.uses + 1)
            if m >= 4 or mode != "first":
                act.wait_ge(c_gw, N(4))
            act.activation(g_raw[m % 4], f1[m % 4][:, 0:S], ACT.Gelu, bias=pk[:, 8 + m:9 + m])\
                .then_inc(c_gl, 1)

        def c_slot_dve(dve, a, m, mode, b):
            new = mode != "tail"
            N = lambda k: a.pairs + (m - k) + 1
            if m == 3 and mode != "first":
                residual(dve, c_f2, a.pairs, c_xr, b - 1, a.biases)
            if mode == "tail" and m == 0:
                a_qk_dve(dve, 0, a.uses + 1)
            if new:
                if m == 7:
                    ln_lo(dve, a.lns + 1)
                dve.wait_ge(c_gl, N(0))
                if m >= 4 or mode != "first":
                    dve.wait_ge(c_f2, N(4))
                dve.tensor_copy(g_hi[m % 4], g_raw[m % 4]).then_inc(c_gh, 1)
                if m == 1:
                    ln_stats(dve, following(b, mode), a.lns + 1)
                if m == 3:
                    ln_apply(dve, following(b, mode), a.lns + 1)
                if m == 5:
                    if mode == "last":
                        dve.wait_ge(pn_in, a.l * 16 + 32)
                    ln_raw(dve, 0 if mode == "last" else 2, a.uses + 1)

        def c_slot_pool(pool, a, m, mode, b):
            N = lambda k: a.pairs + (m - k) + 1
            if m == 2:
                ln_rstd(pool, a.lns + 1)
            pool.wait_ge(c_gh, N(0))
            pool.tensor_tensor(g_lo[m % 4], g_raw[m % 4], f(g_hi[m % 4]), ALU.subtract).then_inc(c_gw, 1)
            if m == 5:
                pool.wait_ge(ln_nm, a.lns + 1)
                add_bias(pool, b, 2)

        def run(eng, stage, l, bar, pre, slot, slots, tails):
            def at(b):
                return At(eng, l, b, stage)
            a = at(0)
            pre(a)
            for i in range(slots):
                slot(a, i, "first", 0)
            with eng.Fori(1, B - 1) as b:
                a = at(b)
                for i in range(slots):
                    slot(a, i, "steady", b)
            a = at(B - 1)
            for i in range(slots):
                slot(a, i, "last", B - 1)
            a = at(B)
            for i in range(tails):
                slot(a, i, "tail", B)
            barrier(eng, bar)

        ctx_raw0 = prob[:, :, :].rearrange("p m n -> p (m n)")[:, 0:CW]
        ctx_raw1 = brow[:, :, :].rearrange("p m n -> p (m n)")[:, 0:CW]

        KOH, PAIRC = 312, 4 * KC
        END = 3 * L
        G_COLS = HF * KOH
        VO_AT = 2 * G_COLS
        MB = brow[:, :, :].rearrange("p m n -> p (m n)")[:, 0:B * KC]
        GB = xres[:, B, :, :]
        yout = otr
        landing = [landed[:, 3 * CH:4 * CH], staged[:, :], prob[:, :, :].rearrange("p m n -> p (m n)"),
                   *(landed[:, i * CH:(i + 1) * CH] for i in (0, 1, 2, 4, 5))]
        NLAND = len(landing)
        FINAL_ORDER = ([("w", 0), ("w", 1), ("u", 0), ("u", 1), ("w", 2), ("u", 2), ("u", 3), ("w", 3), ("u", 4),
                        ("u", 5), ("w", 4), ("w", 5), ("u", 6), ("u", 7), ("w", 6), ("w", 7), ("u", 8), ("u", 9),
                        ("w", 8), ("w", 9), ("u", 10), ("u", 11), ("w", 10), ("w", 11)]
                       + [("u", u) for u in range(12, 16)])

        def span(a, n):
            return slice(a, a + n) if isinstance(a, int) else bass.ds(a, n)

        def final_sync(sp):
            for i in range(12):
                if i == 0:
                    sp.wait_ge(met, 4 * (END - 1))
                if i == 1:
                    sp.wait_ge(w_lo, NSTREAM)
                if i == 2:
                    sp.wait_ge(met, 4 * END)
                if i >= NLAND:
                    sp.wait_ge(w_lo, NSTREAM + i - NLAND + 1)
                sp.dma_start(landing[i % NLAND], wts[NSTREAM + i, :, :]).then_inc(f_in[i % NLAND], 16)
            sp.wait_ge(w_lo, NSTREAM + 10)
            sp.dma_start(staged[:, 0:B * KC].bitcast(I32), mask.rearrange("b k -> (b k)").partition_broadcast(P))\
                .then_inc(f_ms, 16)
            sp.dma_start(GB, rows_f.rearrange("r c -> (r c)").partition_broadcast(P)
                         .rearrange("p (r c) -> p r c", r=2)).then_inc(f_ms, 16)
            with sp.Fori(0, B) as b:
                sp.wait_ge(f_y, b + 1)
                sp.dma_start(out[bass.ds(b, 1), :, :].rearrange("o (q p) c -> p (o q) c", p=P), yout[:, :, :])\
                    .then_inc(out_done, 16)
            sp.wait_ge(out_done, 16 * B + 16)

        def unit_evac_act(act, u, n, dst):
            act.wait_ge(f_ab, u + 1)
            act.activation(dst[0], f1[u % 4][:, 0:n], ACT.Copy).then_inc(f_ah, 1)

        def unit_evac_dve(dve, u, n, dst):
            dve.wait_ge(f_ah, u + 1)
            dve.tensor_tensor(dst[1], f1[u % 4][:, 0:n], f(dst[0]), ALU.subtract).then_inc(f_al, 1)

        def product_dst(u):
            base = 4096 * (u // 8) + (u % 8) * 512
            return cols(W1, base, base + 512)

        def chunk_dst(i):
            j = (i - 4) // 2
            at = i * CH if i < 4 else (j * CH if i % 2 == 0 else 4096 + j * CH)
            return cols(W0, at, at + CH)

        def g_dst(i):
            h, c = i // 2, i % 2
            return cols(W0, c * G_COLS + h * KOH, c * G_COLS + (h + 1) * KOH)

        def vo_dst(i):
            return [w[0:KC, VO_AT + i * 512:VO_AT + (i + 1) * 512] for w in W0]

        def halves(eng, before, slot):
            for hb in range(2):
                before(hb)
                for k in range(4):
                    slot(4 * hb, 0, k, "first")
                with eng.Fori(1, 4) as b4:
                    t = eng.snap(b4 + hb * 4)
                    for k in range(4):
                        slot(t, b4, k, "steady")
                for k in range(4):
                    slot(4 * hb + 4, 4, k, "tail")

        def final_pe(pe):
            def turn(t):
                pe.wait_ge(f_xc, t + 1)
                for c in range(2):
                    for q in range(2):
                        last = pe.transpose(pj[:, c * S + q * P:c * S + (q + 1) * P],
                                            norm[:, q, c * P:(c + 1) * P], ident[:, :])
                last.then_inc(f_tt, 1)
            turn(0)
            for u in range(16):
                h, second = u % 8, u // 8
                pe.wait_ge(w_lo, NSTREAM + (4 + 2 * (h // 2) + 2 if second else h // 2 + 1))
                if u >= 4:
                    pe.wait_ge(f_al, u - 3)
                for e in range(2):
                    for dc in range(2):
                        w = h * 512 + dc * 256
                        last = mm3(pe, f1[u % 4][:, e * 256:(e + 1) * 256],
                                   cols(W0, w + e * P, w + (e + 1) * P), cols(W0, 4096 + w, 4096 + w + 256),
                                   dc == 0, dc == 1)
                last.then_inc(f_ab, 1)

            def before(hb):
                if hb:
                    pe.wait_ge(f_mb, 16)
                    pe.wait_ge(f_pl, 16)
                for i in range(16):
                    u = 16 + 16 * hb + i
                    h, c = i // 2, i % 2
                    pe.wait_ge(f_al, u - 3)
                    if u == 16:
                        pe.wait_ge(f_al, 16)
                    w, k = h * 512 + c * P, slice(hb * KOH, (hb + 1) * KOH)
                    mm3(pe, f1[u % 4][:, 0:KOH], cols(W1, w, w + P), (cTh[:, 0, k], cTl[:, 0, k]), True, False)
                    last = mm2_rest(pe, f1[u % 4][:, 0:KOH], cols(W1, w + 256, w + 256 + P), (cTh[:, 1, k], None),
                                    True, "moving")
                    last.then_inc(f_ab, 1)
                pe.wait_ge(f_al, 32 + 16 * hb)

            def slot(t, b4, k, mode):
                new, old = mode != "tail", (lambda j: k - j >= 0 or mode != "first")
                N = lambda j: t * 4 + (k - j) + 1
                if new:
                    if k == 0:
                        pe.wait_ge(f_tl, t + 1)
                    if old(2):
                        pe.wait_ge(f_mb, N(2))
                    q, hh, m = k % 2, k // 2, k % 2
                    for c in range(2):
                        g = [w[:, c * G_COLS + hh * 4 * KOH:c * G_COLS + (hh + 1) * 4 * KOH]
                             .rearrange("p (h n) -> p h n", h=4)[:, :, span(b4 * KP, KP)] for w in W0]
                        last = mm3(pe, sc[m][:, 0:KOH],
                                   (hTh[:, c, q * P:(q + 1) * P], hTl[:, c, q * P:(q + 1) * P]), g,
                                   c == 0, c == 1)
                    last.then_inc(f_sc, 1)
                if old(1) and (new or k < 1):
                    m = (k - 1) % 2
                    pe.wait_ge(f_nm, N(1))
                    if old(3):
                        pe.wait_ge(f_pl, N(3))
                    for h in range(4):
                        last = pe.transpose(pt[m][0:KC, h * P:(h + 1) * P],
                                            prob[:, m, h * KC:(h + 1) * KC], ident[:, :])
                    last.then_inc(f_tp, 1)
                if new:
                    if k == 0:
                        pe.wait_ge(ctx_b, t + L * B + 1)
                    if old(2):
                        pe.wait_ge(fv_al, N(2))
                    m = [[w[:, 4096 + k * 1024:4096 + (k + 1) * 1024].rearrange("p (h e c) -> p h e c", h=2, e=2)
                          [:, :, e, :] for w in W1] for e in range(2)]
                    mm3(pe, pv[k % 2][0:KC, :], (cbh[:, 0, 0:KC], cbl[:, 0, 0:KC]), m[0], True, False)
                    last = mm2_rest(pe, pv[k % 2][0:KC, :], (cbh[:, 1, 0:KC], None), m[1], True, "stationary")
                    last.then_inc(fv_ab, 1)
                if old(2) and (new or k < 2):
                    kk = (k - 2) % 4
                    q, hh, m = kk % 2, kk // 2, kk % 2
                    pe.wait_ge(f_pl, N(2))
                    pe.wait_ge(fv_al, t * 4 - (4 if k < 2 else 0) + 2 * hh + 2)
                    if kk == 0 and (mode != "first" or t):
                        pe.wait_ge(f_xr, t)
                    for h in range(4):
                        w = VO_AT + (hh * 4 + h) * 256
                        last = mm3(pe, po[:, q * C:(q + 1) * C],
                                   (pth[0:KC, m, h * P:(h + 1) * P], ptl[0:KC, m, h * P:(h + 1) * P]),
                                   [x_[0:KC, w:w + 256] for x_ in W0],
                                   kk == 0 and h == 0, hh == 1 and h == 3, lint=True)
                    last.then_inc(f_op, 1)
                if new and k == 2:
                    pe.wait_ge(f_tl, t + 1)
                    turn(t + 1)
            halves(pe, before, slot)

        def final_act(act):
            def x_hi(t):
                act.wait_ge(f_tt, t + 1)
                act.activation(hTh[:, :, :], pj[:, :].rearrange("p (c n) -> p c n", c=2), ACT.Copy).then_inc(f_th, 1)
            x_hi(0)
            for what, i in FINAL_ORDER:
                if what == "u":
                    unit_evac_act(act, i, 512, product_dst(i))
                    continue
                act.wait_ge(f_in[i % NLAND], 16 * (i // NLAND + 1))
                if i >= 4:
                    act.wait_ge(f_ab, 2 * ((i - 4) // 2) + 2)
                act.activation(chunk_dst(i)[0], landing[i % NLAND], ACT.Copy).then_inc(w_hi, 2)

            def before(hb):
                act.wait_ge(f_ab, 16)
                if hb:
                    act.wait_ge(f_sc, 16)
                for i in range(16):
                    unit_evac_act(act, 16 + 16 * hb + i, KOH, g_dst(i))

            def slot(t, b4, k, mode):
                new, old = mode != "tail", (lambda j: k - j >= 0 or mode != "first")
                N = lambda j: t * 4 + (k - j) + 1
                if old(1) and (new or k < 1):
                    m = (k - 1) % 2
                    act.wait_ge(f_tp, N(1))
                    if old(3):
                        act.wait_ge(f_op, N(3))
                    act.activation(pth[0:KC, m, :], pt[m][0:KC, :], ACT.Copy).then_inc(f_ph, 1)
                if not new:
                    return
                if k == 3:
                    act.wait_ge(f_sc, N(0))
                    x_hi(t + 1)
                m = k % 2
                act.wait_ge(f_nb, N(0))
                for h in range(4):
                    v = prob[:, m, h * KC:(h + 1) * KC]
                    last = act.activation(v, v, ACT.Exp, bias=nbias[:, m, h:h + 1], scale=SCALE_F,
                                          accum_out=psums[:, m, h:h + 1])
                last.then_inc(f_ex, 1)
                act.wait_ge(fv_ab, N(0))
                if mode != "first" or t:
                    act.wait_ge(f_op, t * 4 - (2 if k < 2 else 0))
                act.activation(vo_dst(k)[0], pv[k % 2][0:KC, :], ACT.Copy).then_inc(fv_ah, 1)
            halves(act, before, slot)

        def final_dve(dve):
            def x_copy(t):
                dve.tensor_copy(norm[:, :, :], xs(t)).then_inc(f_xc, 1)

            def x_lo(t):
                dve.wait_ge(f_th, t + 1)
                dve.tensor_tensor(hTl[:, :, :], pj[:, :].rearrange("p (c n) -> p c n", c=2), f(hTh[:, :, :]),
                                  ALU.subtract).then_inc(f_tl, 1)
            x_copy(0)
            x_lo(0)
            for what, i in FINAL_ORDER:
                if what == "u":
                    unit_evac_dve(dve, i, 512, product_dst(i))
                    continue
                hi, lo = chunk_dst(i)
                dve.wait_ge(w_hi, 2 * (NSTREAM + i + 1))
                dve.tensor_tensor(lo, landing[i % NLAND], f(hi), ALU.subtract).then_inc(w_lo, 1)
            zeros = prob[:, :, :].rearrange("p m n -> p (m n)")[:, 0:B * KC]
            dve.memset(MB, float("-inf")).then_inc(f_mb0, 1)
            dve.memset(zeros, 0.0).then_inc(f_mb0, 1)
            dve.wait_ge(f_ms, 32)
            dve.wait_ge(f_mb0, 2)
            dve.copy_predicated(MB, staged[:, 0:B * KC].bitcast(I32), zeros).then_inc(f_mb0, 1)

            def before(hb):
                for i in range(16):
                    unit_evac_dve(dve, 16 + 16 * hb + i, KOH, g_dst(i))
                dve.wait_ge(f_mb0, 3)

            def slot(t, b4, k, mode):
                new, old = mode != "tail", (lambda j: k - j >= 0 or mode != "first")
                N = lambda j: t * 4 + (k - j) + 1
                if old(1) and (new or k < 1):
                    m = (k - 1) % 2
                    dve.wait_ge(f_ex, N(1))
                    dve.reciprocal(rsum[:, m, :], psums[:, m, :]).then_inc(f_rc, 1)
                    dve.wait_ge(fv_ah, N(1))
                    hi, lo = vo_dst((k - 1) % 4)
                    dve.tensor_tensor(lo, pv[m][0:KC, :], f(hi), ALU.subtract).then_inc(fv_al, 1)
                if new and k == 0:
                    if mode == "first" and t == 0:
                        context_to_fixed(dve, t, w_lo, NCHUNK)
                    else:
                        context_to_fixed(dve, t, fv_al, t * 4)
                if new:
                    m = k % 2
                    dve.wait_ge(f_sc, N(0))
                    if old(2):
                        dve.wait_ge(f_tp, N(2))
                    v = prob[:, m, 0:PAIRC].rearrange("p (h k) -> p h k", h=4)
                    bias = MB[:, span(t * KC, KC)].unsqueeze(1).to_broadcast([P, 4, KC])
                    dve.tensor_tensor(v, sc[m][:, 0:KOH].rearrange("p (h k) -> p h k", h=4)[:, :, 0:KC],
                                      bias, ALU.add).then_inc(f_mb, 1)
                    dve.wait_ge(f_mb, N(0))
                    dve.tensor_reduce(nmax[:, m, :], v, AX.X, ALU.max, negate=True).then_inc(f_mx, 1)
                    dve.wait_ge(f_mx, N(0))
                    dve.tensor_scalar(nbias[:, m, :], nmax[:, m, :], SCALE_F, None, ALU.mult)\
                        .then_inc(f_nb, 1)
                if k == 2 and mode != "first":
                    dve.wait_ge(f_op, t * 4)
                    dve.tensor_tensor(xs(t - 1), po[:, :].rearrange("p (q c) -> p q c", q=2), xs(t - 1), ALU.add)\
                        .then_inc(f_xr, 1)
                if old(1) and (new or k < 1):
                    m = (k - 1) % 2
                    dve.wait_ge(f_ph, N(1))
                    dve.tensor_tensor(ptl[0:KC, m, :], pt[m][0:KC, :], f(pth[0:KC, m, :]), ALU.subtract)\
                        .then_inc(f_pl, 1)
                if new and k == 0:
                    dve.wait_ge(f_tt, t + 1)
                    x_copy(t + 1)
                if new and k == 3:
                    x_lo(t + 1)
                if k == 2 and mode != "first":
                    dve.wait_ge(f_xr, t)
                    dve.memset(pace[:, :], 0.0)
                    for q in range(2):
                        last = dve.bn_stats(stats[:, q, :], xs(t - 1)[:, q, :])
                    last.then_inc(f_st, 1)
                    dve.wait_ge(f_st, t)
                    dve.memset(pace[:, :], 0.0)
                    for q in range(2):
                        last = dve.bn_aggr(mv[:, q, :], stats[:, q, :])
                    last.then_inc(ln_mv, 1)
                    dve.wait_ge(ln_mv, t + 24 * L + 1)
                    dve.wait_ge(out_done, t * 16)
                    for q in range(2):
                        last = dve.scalar_tensor_tensor(yout[:, q, :], xs(t - 1)[:, q, :], mv[:, q, 0:1],
                                                        GB[:, 0, :], ALU.subtract, ALU.mult)
                    last.then_inc(f_xn, 1)
                if k == 3 and mode != "first":
                    dve.wait_ge(ln_rs, t + 24 * L + 1)
                    dve.wait_ge(f_xn, t)
                    for q in range(2):
                        last = dve.scalar_tensor_tensor(yout[:, q, :], yout[:, q, :], rstd[:, q:q + 1],
                                                        GB[:, 1, :], ALU.mult, ALU.add)
                    last.then_inc(f_y, 1)
            halves(dve, before, slot)

        def final_pool(pool):
            def slot(t, b4, k, mode):
                new, old = mode != "tail", (lambda j: k - j >= 0 or mode != "first")
                if old(1) and (new or k < 1):
                    m = (k - 1) % 2
                    v = prob[:, m, 0:PAIRC].rearrange("p (h k) -> p h k", h=4)
                    pool.wait_ge(f_rc, t * 4 + k)
                    pool.tensor_tensor(v, v, rsum[:, m, :].unsqueeze(2).to_broadcast([P, 4, KC]), ALU.mult)\
                        .then_inc(f_nm, 1)
                if k == 3 and mode != "first":
                    ln_rstd(pool, t + 24 * L)
            halves(pool, lambda hb: None, slot)

        block = ctx.enter_context(nc.Block())

        @block.sync
        def _(sp):
            sp.sem_inc(out_done, 16)
            xin = x.rearrange("b (q p) c -> p b q c", p=P)
            sp.dma_start(xres[:, 0:1, :, :], xin[:, 0:1, :, :]).then_inc(x_in, 16)
            sp.dma_start(staged[:, :], wts[0, :, :]).then_inc(stg_in, 16)
            sp.dma_start(landed[:, 4 * CH:5 * CH], wts[1, :, :]).then_inc(first_in[0], 16)
            for e, raw in enumerate((ctx_raw0, ctx_raw1)):
                sp.dma_start(raw, ctx_t[e, :, :]).then_inc(ctx_in, 16)
            sp.dma_start(landed[:, 5 * CH:6 * CH], wts[2, :, :]).then_inc(first_in[1], 16)
            sp.dma_start(landed[:, 3 * CH:4 * CH], wts[3, :, :]).then_inc(first_in[2], 16)
            sp.dma_start(xres[:, 1:B, :, :], xin[:, 1:B, :, :]).then_inc(x_rest, 16)
            sp.wait_ge(w_lo, 1)
            sp.dma_start(staged[:, :], wts[NA_HIGH, :, :]).then_inc(stg_in, 16)
            with sp.Fori(NA_HIGH + 1, NSTREAM) as k:
                sp.wait_ge(w_lo, k)
                sp.dma_start(staged[:, :], wts[bass.ds(k, 1), :, :].rearrange("o p n -> p (o n)"))\
                    .then_inc(stg_in, 16)
            final_sync(sp)

        def layers(eng, body):
            with eng.Fori(0, L) as l:
                body(l)

        @block.tensor
        def _(pe):
            pe.wait_ge(setup_g, 2)
            ln_turn(pe, 1, 0, vb, v_full, v_free)
            pe.wait_ge(w_lo, 1)
            a_qk_pe(pe, 0, 1, 1)
            pe.wait_ge(w_lo, 2)
            a_v_pe(pe, A_V[15], 2, 1)

            def body(l):
                def a_slot(a, h, mode, b):
                    if mode == "first":
                        need = {2: 3, 6: 4, 7: NA_HIGH + 2, 10: NA_HIGH + 3, 15: NA_HIGH + 4}
                        if h in need:
                            pe.wait_ge(w_lo, l * PER_LAYER + need[h])
                    a_slot_pe(pe, a, h, mode)
                run(pe, 0, l, 3 * l + 1, lambda a: None, a_slot, H, 6)

                run(pe, 1, l, 3 * l + 2, lambda a: None, lambda a, p, mode, b: b_slot_pe(pe, a, p, mode, b), NPAIR, 5)

                run(pe, 2, l, 3 * l + 3, lambda a: None,
                    lambda a, m, mode, b: c_slot_pe(pe, a, m, mode), 8, 3)
            layers(pe, body)
            final_pe(pe)

        @block.scalar
        def _(act):
            def params(l):
                act.dma_start(pk[:, :], par[bass.ds(l, 1), :, 4:20].rearrange("o p n -> p (o n)"))\
                    .then_inc(par_in, 16)
                act.dma_start(brow[:, :, :], rows[bass.ds(l, 1), :, :].rearrange("o r c -> (o r c)")
                              .partition_broadcast(P).rearrange("p (r c) -> p r c", r=3))\
                    .then_inc(par_in, 16)

            act.dma_start(pn[:, :], par[0, :, 0:4]).then_inc(pn_in, 16)
            for k in (1, 2, 3):
                act.wait_ge(first_in[k - 1], 16)
                if k == 1:
                    act.wait_ge(w_hi, 2)
                act.activation(first_dst(k)[0], landing[(None, 6, 7, 0)[k]], ACT.Copy).then_inc(w_hi, 2)
                if k == 1:
                    ln_hi(act, 1, v_free)
            a_qk_act(act, 0, 1)
            a_v_act(act, A_V[15], 2)
            act.wait_ge(setup_g, 4)
            act.activation(cTh[64:P, 1, :], f(cTl[64:P, 1, :]), ACT.Copy).then_inc(setup_g, 1)

            def body(l):
                params(l)

                run(act, 0, l, 3 * l + 1, lambda a: None, lambda a, h, mode, b: a_slot_act(act, a, h, mode), H, 3)

                def pre_b(a):
                    act.dma_start(pn[:, :], par[bass.ds(l + 1, 1), :, 0:4].rearrange("o p n -> p (o n)"))\
                        .then_inc(pn_in, 16)
                run(act, 1, l, 3 * l + 2, pre_b, lambda a, p, mode, b: b_slot_act(act, a, p, mode), NPAIR, 3)

                run(act, 2, l, 3 * l + 3, lambda a: None,
                    lambda a, m, mode, b: c_slot_act(act, a, m, mode), 8, 2)
            layers(act, body)
            final_act(act)

        @block.vector
        def _(dve):
            dve.sem_inc(pj_free, GIVEN)
            dve.sem_inc(v_free, GIVEN)
            dve.sem_inc(ln_hT, GIVEN)
            dve.memset(half[:, :], -0.5).then_inc(setup_v, 1)
            dve.memset(ones[:, :], 1.0).then_inc(setup_v, 1)
            dve.memset(eps[:, :], EPS).then_inc(setup_v, 1)
            dve.wait_ge(x_in, 16)
            dve.wait_ge(setup_v, 3)
            ln_stats(dve, 0, 0)
            dve.wait_ge(stg_in, 16)
            hi, lo = first_dst(0)
            dve.tensor_copy(hi, staged[:, :]).then_inc(w_hi, 2)
            dve.wait_ge(w_hi, 2)
            dve.tensor_tensor(lo, staged[:, :], f(hi), ALU.subtract).then_inc(w_lo, 1)
            ln_apply(dve, 0, 0)
            dve.wait_ge(pn_in, 16)
            ln_raw(dve, 0, 1, vb, v_full, v_hi, v_free)
            ln_lo(dve, 0)
            dve.wait_ge(w_hi, 4)
            dve.tensor_tensor(first_dst(1)[1], landing[6], f(first_dst(1)[0]), ALU.subtract).then_inc(w_lo, 1)
            a_qk_dve(dve, 0, 1)

            def body(l):
                run(dve, 0, l, 3 * l + 1, lambda a: None,
                    lambda a, h, mode, b: a_slot_dve(dve, a, h, mode, b), H, 7)

                run(dve, 1, l, 3 * l + 2, lambda a: None,
                    lambda a, p, mode, b: b_slot_dve(dve, a, p, mode, b), NPAIR, 6)

                run(dve, 2, l, 3 * l + 3, lambda a: None,
                    lambda a, m, mode, b: c_slot_dve(dve, a, m, mode, b), 8, 4)
            layers(dve, body)
            final_dve(dve)

        @block.gpsimd
        def _(pool):
            pool.memset(ident[:, :], 0.0).then_inc(setup_g, 1)
            pool.wait_ge(setup_g, 1)
            pool.affine_select(out=ident[:, :], in_=ident[:, :], compare_op=ALU.not_equal, fill=1.0, base=0,
                               pattern=[[-1, P]], channel_multiplier=1).then_inc(setup_g, 1)
            ln_rstd(pool, 0)
            pool.wait_ge(ctx_in, 32)
            for e, raw in enumerate((ctx_raw0, ctx_raw1)):
                last = pool.tensor_scalar(cTh[:, e, :], raw, 1.0, 1.0, ALU.mult, ALU.mult)
            last.then_inc(setup_g, 1)
            pool.wait_ge(setup_g, 3)
            for e, raw in enumerate((ctx_raw0, ctx_raw1)):
                last = pool.tensor_tensor(cTl[:, e, :], raw, f(cTh[:, e, :]), ALU.subtract)
            last.then_inc(setup_g, 1)
            pool.wait_ge(w_lo, 2)
            for k in (2, 3):
                pool.wait_ge(w_hi, 2 * k + 2)
                hi, lo = first_dst(k)
                pool.tensor_tensor(lo, landing[(None, 6, 7, 0)[k]], f(hi), ALU.subtract).then_inc(w_lo, 1)

            def body(l):
                run(pool, 0, l, 3 * l + 1, lambda a: None,
                    lambda a, h, mode, b: a_slot_pool(pool, a, h, mode, b, l), H, 4)
                run(pool, 1, l, 3 * l + 2, lambda a: None,
                    lambda a, p, mode, b: b_slot_pool(pool, a, p, mode, b, l), NPAIR, 4)

                run(pool, 2, l, 3 * l + 3, lambda a: None,
                    lambda a, m, mode, b: c_slot_pool(pool, a, m, mode, b), 8, 0)
            layers(pool, body)
            final_pool(pool)


def _chunks(v):
    import numpy as np

    def tiles(w, n):
        if w.shape[0] == 192:
            w = np.concatenate([w, w[128:]])
        r = w.shape[0] // 128
        return w.reshape(r, 128, -1, n).transpose(1, 0, 2, 3)

    def a_chunks(l):
        w = v["L0_xattn_w_qkv"][l]
        q, k, vv = w[:, 0:1024], w[:, 1024:2048], w[:, 2048:3072]
        qk = np.stack([tiles(q, 128), tiles(k, 128)], axis=0).transpose(1, 3, 0, 2, 4)
        vg = tiles(vv, 256).transpose(0, 2, 1, 3)
        o = tiles(v["L0_xattn_w_sa_o"][l], 256)
        o = o.reshape(128, 2, 1024)
        qk = qk.reshape(128, 4, 1024)
        vg = vg.reshape(128, 2, 1024)
        low = [o[:, 0], vg[:, 1], qk[:, 3], o[:, 1]]
        high = [qk[:, 0], vg[:, 0], qk[:, 1], qk[:, 2]]
        return low, high

    def b_chunks(l):
        w = v["L0_xattn_w_kv"][l]
        q = tiles(v["L0_xattn_w_q"][l], 128).transpose(0, 2, 1, 3).reshape(128, 2, 1024)
        k = tiles(w[:, 0:1024], 128).transpose(0, 2, 1, 3).reshape(128, 2, 1024)
        vv = tiles(w[:, 1024:2048], 256).transpose(0, 2, 1, 3).reshape(128, 2, 1024)
        o = tiles(v["L0_xattn_w_ca_o"][l], 256).reshape(128, 2, 1024)
        return [t[:, i] for t in (q, k, vv, o) for i in range(2)]

    def c_chunks(l):
        w1 = tiles(v["L0_xattn_w_ff1"][l], 128).transpose(0, 2, 1, 3).reshape(128, 2, 1024)
        w2 = tiles(v["L0_xattn_w_ff2"][l], 256).reshape(128, 2, 1024)
        return [t[:, i] for t in (w1, w2) for i in range(2)]

    def by_head(w):
        if w.shape[0] == 192:
            w = np.concatenate([w, w[128:]])
        return w.reshape(256, 8, 2, 128).transpose(3, 1, 2, 0).reshape(128, 4, 1024)

    wq, wk, wv = (by_head(v[f"L1_xattn_W{n}"]) for n in "qkv")
    wo = v["L1_xattn_Wo"].reshape(8, 2, 128, 256).transpose(2, 0, 1, 3).reshape(128, 4, 1024)
    n_layers = v["L0_xattn_w_qkv"].shape[0]
    out = list(a_chunks(0)[1])
    for l in range(n_layers):
        out += a_chunks(l)[0] + b_chunks(l) + c_chunks(l)
        out += a_chunks(l + 1)[1] if l + 1 < n_layers else [wq[:, i] for i in range(4)]
    out += [wk[:, i] for i in range(4)]
    for i in range(4):
        out += [wv[:, i], wo[:, i]]
    return np.ascontiguousarray(np.stack(out))


def kernel(**inputs):
    import numpy as np
    import concourse.bacc as bacc
    from concourse.bass_utils import run_bass_kernel_spmd

    v = {k: np.asarray(a) for k, a in inputs.items()}
    n = lambda name: v["L0_xattn_" + name]
    ctx_t = np.zeros((2, 128, B, KP), v["ctx_768"].dtype)
    c = v["ctx_768"].transpose(2, 0, 1)
    ctx_t[0, :, :, :KC] = c[0:128]
    ctx_t[1, 0:64, :, :KC] = c[128:192]
    ctx_t[1, 64:128, :, :KC] = c[128:192]
    column = lambda a: a.reshape(L, -1, 128).transpose(0, 2, 1)
    par = np.concatenate([column(n(m)) for i in (1, 2, 3) for m in (f"ln{i}_g", f"ln{i}_b")]
                         + [column(n("b_ff1"))], axis=2)
    par = np.concatenate([par, par[:1]])
    rows = np.stack([n("b_sa_o"), n("b_ca_o"), n("b_ff2")], axis=1)
    arrays = {
        "x": v["x"], "ctx_t": ctx_t.reshape(2, 128, CW), "mask": v["mask_BxS2_if1"], "wts": _chunks(v),
        "par": par, "rows": rows, "rows_f": np.stack([v["L1_xattn_gamma"], v["L1_xattn_beta"]]),
    }
    arrays = {k: np.ascontiguousarray(a) for k, a in arrays.items()}
    nc = bacc.Bacc("TRN2", target_bir_lowering=False, num_devices=1)
    args = [nc.dram_tensor(f"in_{k}", a.shape, mybir.dt.from_np(a.dtype), kind="ExternalInput").ap()
            for k, a in arrays.items()]
    out = nc.dram_tensor("out_y", (B, S, C), F32, kind="ExternalOutput").ap()
    build(nc, *args, out)
    r = run_bass_kernel_spmd(nc, [{f"in_{k}": a for k, a in arrays.items()}], core_ids=[0])
    return r.results[0]["out_y"]
```
